# Optimizing a Trainium2 kernel written in Bass

```python
import numpy as np
import jax
import jax.numpy as jnp

def _softmax(x, axis=-1):
    return jax.nn.softmax(x, axis=axis)

def _gelu(x):
    return jax.nn.gelu(x, approximate=True)

def _silu(x):
    return jax.nn.silu(x)

def _sigmoid(x):
    return jax.nn.sigmoid(x)

def _layernorm(x, axis=-1, eps=1e-05):
    m = jnp.mean(x, axis=axis, keepdims=True)
    v = jnp.var(x, axis=axis, keepdims=True)
    return (x - m) / jnp.sqrt(v + eps)

def _scatter_add(tgt, idx, src, axis=0):
    return tgt.at[idx].add(src)

def _segment_sum(src, seg, n):
    return jax.ops.segment_sum(src, seg, n)
kernel_name = 'mk_conv_attn_hybrid_d2_conv_nchw512_r4_e4db18'

def setup_inputs(seed: int=0):
    np.random.seed(seed)
    _w = jnp.asarray

    def _rec_inputs():
        import jax
        import jax.numpy as jnp
        _gk = jax.random.key(seed)
        x = 0.03137 + 0.2501 * jax.random.normal(jax.random.fold_in(_gk, 1), (16, 128, 32, 32), jnp.float32)
        return x
    x = _rec_inputs()

    def _L0_conv_setup():
        import jax, jax.numpy as jnp
        import numpy as np
        EPS_LOG = 1e-08

        def _log_eig(Xf):
            w, V = jnp.linalg.eigh(Xf)
            w = jnp.clip(w, EPS_LOG)
            return jnp.einsum('nij,nj,nkj->nik', V, jnp.log(w), V)

        def _exp_eig(Lc):
            w, V = jnp.linalg.eigh(Lc)
            return jnp.einsum('nij,nj,nkj->nik', V, jnp.exp(w), V)
        key = jax.random.key(seed)
        B, K, s = (16, 128, 32)
        A = jax.random.normal(key, (B, K, s, s), dtype=jnp.float32)
        X = jnp.einsum('bkij,bklj->bkil', A, A) / s + 0.001 * jnp.eye(s, dtype=jnp.float32)
        gamma = jnp.ones((1,), dtype=jnp.float32)
        beta = jnp.zeros((1,), dtype=jnp.float32)
        return {'X': X, 'gamma': gamma, 'beta': beta}
    _L0_conv_all = _L0_conv_setup()
    _L0_conv_in = {k: v for k, v in _L0_conv_all.items() if k in ('gamma', 'beta')}
    del _L0_conv_all

    def _L1_attn_setup():
        import jax, jax.numpy as jnp
        import numpy as np
        HEADS = 8
        DIM_HEAD = 16
        TOPK = 32
        SCALE = DIM_HEAD ** (-0.5)
        key = jax.random.key(seed)
        ks = jax.random.split(key, 6)
        b, n, d = (2, 1024, 128)
        inner = HEADS * DIM_HEAD
        x = jax.random.normal(ks[0], (b, n, d), dtype=jnp.float32)
        Wq = jax.random.normal(ks[1], (d, inner), dtype=jnp.float32) * 0.02
        Wk = jax.random.normal(ks[2], (d, inner), dtype=jnp.float32) * 0.02
        Wv = jax.random.normal(ks[3], (d, inner), dtype=jnp.float32) * 0.02
        Wo = jax.random.normal(ks[4], (inner, d), dtype=jnp.float32) * 0.02
        bo = jnp.zeros((d,), dtype=jnp.float32)
        return {'x': x, 'Wq': Wq, 'Wk': Wk, 'Wv': Wv, 'Wo': Wo, 'bo': bo}
    _L1_attn_all = _L1_attn_setup()
    _L1_attn_in = {k: v for k, v in _L1_attn_all.items() if k in ('Wq', 'Wk', 'Wv', 'Wo', 'bo')}
    del _L1_attn_all

    def _L1_ffn_setup():
        import jax, jax.numpy as jnp
        import numpy as np
        B, T, H = (8, 2048, 128)
        E, R = (4, 16)
        SCALE = 0.04
        key = jax.random.key(seed)
        ks = jax.random.split(key, 7)
        return {'x': jax.random.normal(ks[0], (B, T, H), jnp.float32), 'gate_w': jax.random.normal(ks[1], (E, H), jnp.float32) * SCALE, 'thr_w': jax.random.normal(ks[2], (1, H), jnp.float32) * SCALE, 'fc1_w': jax.random.normal(ks[3], (E, H, H), jnp.float32) * SCALE, 'lora_A': jax.random.normal(ks[4], (E, H, R), jnp.float32) * SCALE, 'lora_B': jax.random.normal(ks[5], (E, R, H), jnp.float32) * SCALE, 'fc2_w': jax.random.normal(ks[6], (E, H, H), jnp.float32) * SCALE}
    _L1_ffn_all = _L1_ffn_setup()
    _L1_ffn_in = {k: v for k, v in _L1_ffn_all.items() if k in ('gate_w', 'thr_w', 'fc1_w', 'lora_A', 'lora_B', 'fc2_w')}
    del _L1_ffn_all
    return {'x': x, 'L0_conv_gamma': _L0_conv_in['gamma'], 'L0_conv_beta': _L0_conv_in['beta'], 'L1_attn_Wq': _L1_attn_in['Wq'], 'L1_attn_Wk': _L1_attn_in['Wk'], 'L1_attn_Wv': _L1_attn_in['Wv'], 'L1_attn_Wo': _L1_attn_in['Wo'], 'L1_attn_bo': _L1_attn_in['bo'], 'L1_ffn_gate_w': _L1_ffn_in['gate_w'], 'L1_ffn_thr_w': _L1_ffn_in['thr_w'], 'L1_ffn_fc1_w': _L1_ffn_in['fc1_w'], 'L1_ffn_lora_A': _L1_ffn_in['lora_A'], 'L1_ffn_lora_B': _L1_ffn_in['lora_B'], 'L1_ffn_fc2_w': _L1_ffn_in['fc2_w']}

def reference(x, L0_conv_gamma, L0_conv_beta, L1_attn_Wq, L1_attn_Wk, L1_attn_Wv, L1_attn_Wo, L1_attn_bo, L1_ffn_gate_w, L1_ffn_thr_w, L1_ffn_fc1_w, L1_ffn_lora_A, L1_ffn_lora_B, L1_ffn_fc2_w):
    import jax
    import jax.numpy as jnp

    def _L0_conv_ref(X, gamma, beta):
        import jax, jax.numpy as jnp
        import numpy as np
        EPS_LOG = 1e-08

        def _log_eig(Xf):
            w, V = jnp.linalg.eigh(Xf)
            w = jnp.clip(w, EPS_LOG)
            return jnp.einsum('nij,nj,nkj->nik', V, jnp.log(w), V)

        def _exp_eig(Lc):
            w, V = jnp.linalg.eigh(Lc)
            return jnp.einsum('nij,nj,nkj->nik', V, jnp.exp(w), V)
        B, K, s, _ = X.shape
        Xf = X.reshape(B * K, s, s)
        L = _log_eig(Xf)
        mean_log = jnp.mean(L, axis=0)
        Lc = gamma * (L - mean_log) + beta
        Y = _exp_eig(Lc)
        return Y.reshape(B, K, s, s)

    def _L1_attn_ref(x, Wq, Wk, Wv, Wo, bo):
        import jax, jax.numpy as jnp
        import numpy as np
        HEADS = 8
        DIM_HEAD = 16
        TOPK = 32
        SCALE = DIM_HEAD ** (-0.5)
        b, n, _ = x.shape
        h, dh = (HEADS, DIM_HEAD)
        q = (x @ Wq).reshape(b, n, h, dh).transpose(0, 2, 1, 3)
        k = (x @ Wk).reshape(b, n, h, dh).transpose(0, 2, 1, 3)
        v = (x @ Wv).reshape(b, n, h, dh).transpose(0, 2, 1, 3)
        dots = jnp.einsum('bhnd,bhmd->bhnm', q, k) * SCALE
        top_dots, top_inds = jax.lax.top_k(dots, TOPK)
        attn = jax.nn.softmax(top_dots, axis=-1)
        gather_rows = lambda vi, ii: vi[ii]
        vg = jax.vmap(jax.vmap(gather_rows))(v, top_inds)
        out = jnp.einsum('bhnk,bhnkd->bhnd', attn, vg)
        out = out.transpose(0, 2, 1, 3).reshape(b, n, h * dh)
        return out @ Wo + bo

    def _L1_ffn_ref(x, gate_w, thr_w, fc1_w, lora_A, lora_B, fc2_w):
        import jax, jax.numpy as jnp
        import numpy as np
        B, T, H = (8, 2048, 128)
        E, R = (4, 16)
        SCALE = 0.04
        b, t, h = x.shape
        e = gate_w.shape[0]
        xf = x.reshape(-1, h)
        gate_logits = jax.nn.softmax(xf @ gate_w.T, axis=-1)
        thresholds = jax.nn.sigmoid(xf @ thr_w.T) * (1.0 / e)
        adapted = gate_logits - thresholds
        selected = (adapted >= 0).astype(xf.dtype)
        weights = adapted * selected
        wsum = jnp.sum(weights, axis=-1, keepdims=True)
        wsum = jnp.where(wsum == 0, jnp.ones_like(wsum), wsum)
        weights = weights / wsum
        hidden = jax.nn.relu(jnp.einsum('ni,ehi->neh', xf, fc1_w))
        lo = jnp.einsum('neh,ehr->ner', hidden, lora_A)
        lo = jnp.einsum('ner,ero->neo', lo, lora_B)
        expert_out = jnp.einsum('neo,edo->ned', lo, fc2_w)
        out = jnp.einsum('ne,ned->nd', weights, expert_out)
        return out.reshape(b, t, h)

    def _gn(v, G=32, eps=1e-05):
        B_, C_, H_, W_ = v.shape
        g = v.reshape(B_, G, C_ // G, H_, W_)
        m = jnp.mean(g, axis=(2, 3, 4), keepdims=True)
        s = jnp.var(g, axis=(2, 3, 4), keepdims=True)
        return ((g - m) / jnp.sqrt(s + eps)).reshape(v.shape)

    def _ln_c(v, eps=1e-06):
        m = jnp.mean(v, axis=1, keepdims=True)
        s = jnp.var(v, axis=1, keepdims=True)
        return (v - m) / jnp.sqrt(s + eps)

    def _ln_t(v, eps=1e-05):
        m = jnp.mean(v, axis=-1, keepdims=True)
        s = jnp.var(v, axis=-1, keepdims=True)
        return (v - m) / jnp.sqrt(s + eps)

    def _to_tokens(v):
        B_, C_, H_, W_ = v.shape
        return v.reshape(B_, C_, H_ * W_).transpose(0, 2, 1)

    def _from_tokens(t, like):
        B_, C_, H_, W_ = like.shape
        return t.transpose(0, 2, 1).reshape(B_, C_, H_, W_)
    x = x + _L0_conv_ref(_gn(x), L0_conv_gamma, L0_conv_beta)
    t = _to_tokens(x)
    t = t + _L1_attn_ref(_ln_t(t), L1_attn_Wq, L1_attn_Wk, L1_attn_Wv, L1_attn_Wo, L1_attn_bo)
    t = t + _L1_ffn_ref(_ln_t(t), L1_ffn_gate_w, L1_ffn_thr_w, L1_ffn_fc1_w, L1_ffn_lora_A, L1_ffn_lora_B, L1_ffn_fc2_w)
    x = _from_tokens(t, x)
    return x

_drawn_inputs = setup_inputs


def setup_inputs(seed=0):
    import zlib

    import numpy as np

    out = dict(_drawn_inputs(seed))
    spreads = {'L1_attn_bo': (0.0, 2.0)}
    factors = {'L1_attn_Wq': 64.0,
     'L1_attn_Wk': 64.0,
     'L1_attn_Wv': 64.0,
     'L1_attn_Wo': 64.0,
     'L1_ffn_gate_w': 45.855,
     'L1_ffn_thr_w': 64.0,
     'L1_ffn_fc1_w': 45.06,
     'L1_ffn_lora_A': 36.792,
     'L1_ffn_lora_B': 37.3,
     'L1_ffn_fc2_w': 38.863}
    for name, (base, spread) in spreads.items():
        noise = np.random.default_rng([zlib.crc32(name.encode()), seed]).standard_normal(out[name].shape)
        drawn = base * np.exp(spread * noise) if base else spread * noise
        out[name] = jnp.asarray(drawn.astype(out[name].dtype))
    for name, factor in factors.items():
        out[name] = (out[name] * factor).astype(out[name].dtype)
    return out
```

```python
import math
from contextlib import ExitStack

import concourse.bass as bass
from concourse import mybir

F32 = mybir.dt.float32
ALU = mybir.AluOpType
ACT = mybir.ActivationFunctionType
AX = mybir.AxisListType

P = 128
B = 16
S = 32
N = S * S
HB = B // 2
PAIRS = S // 2
ROUNDS = S - 1
SWEEPS = 6
EPS_LOG = 1e-8
GROUP = 4
EPS_GN = 1e-5
TINY = 1e-30
TINY_LOG = 1e-18
SQUARINGS = 7
TAYLOR = [1.0 / math.factorial(n) for n in range(7)]
QUADS = B // 4


class Memory:
    pass


class Count:

    def __init__(self, sem, base=0):
        self.sem, self.base, self.n = sem, base, 0

    def up(self, ins, by=1):
        self.n += by
        ins.then_inc(self.sem, by)
        return self.value()

    def value(self):
        return self.base + self.n


def chained(eng, count, ins):
    hold(eng, count.sem, count.up(ins))


def hold(eng, sem, value):
    eng.wait_ge(sem, value)
    eng.sem_inc(Passed.sem, 1)


class Passed:
    sem = None


def refine_root(nc, eng, sem, at, root, of, spare):
    nc.vector.reciprocal(spare, root).then_inc(sem, 1)
    eng.wait_ge(sem, at + 1)
    nc.vector.tensor_tensor(spare, spare, of, ALU.mult).then_inc(sem, 1)
    eng.wait_ge(sem, at + 2)
    nc.vector.tensor_tensor(root, root, spare, ALU.add).then_inc(sem, 1)
    eng.wait_ge(sem, at + 3)
    nc.vector.tensor_scalar(root, root, 0.5, None, ALU.mult).then_inc(sem, 1)
    eng.wait_ge(sem, at + 4)


def constants(nc, mem):
    with ExitStack() as ctx:
        filled = ctx.enter_context(nc.semaphore("filled"))
        block = ctx.enter_context(nc.Block())

        @block.gpsimd
        def _(pool):
            nc.gpsimd.memset(mem.ident[:], 0.0).then_inc(filled, 1)
            nc.gpsimd.memset(mem.group[:], 1.0 / (GROUP * N)).then_inc(filled, 1)
            nc.gpsimd.memset(mem.quad_mean[:], 0.0).then_inc(filled, 1)
            nc.gpsimd.memset(mem.tiny[:], TINY).then_inc(filled, 1)
            nc.gpsimd.memset(mem.eps_gn[:], EPS_GN).then_inc(filled, 1)
            for tile, value in ((mem.minus_tiny, -TINY), (mem.tiny_log, TINY_LOG), (mem.one, 1.0), (mem.two, 2.0),
                                (mem.half, 0.5)):
                nc.gpsimd.memset(tile[:], value)
            hold(pool, filled, 5)
            nc.gpsimd.affine_select(out=mem.ident[:], in_=mem.ident[:], compare_op=ALU.not_equal, fill=1.0,
                                    base=0, pattern=[[-1, P]], channel_multiplier=1).then_inc(filled, 1)
            gv = mem.group[:].rearrange("p (g c) -> p g c", c=GROUP)
            nc.gpsimd.affine_select(out=gv, in_=gv, compare_op=ALU.is_ge, fill=0.0, base=0,
                                    pattern=[[-GROUP, P // GROUP], [0, GROUP]], channel_multiplier=1).then_inc(filled, 1)
            hold(pool, filled, 7)
            nc.gpsimd.affine_select(out=gv, in_=gv, compare_op=ALU.is_ge, fill=0.0, base=GROUP - 1,
                                    pattern=[[GROUP, P // GROUP], [0, GROUP]], channel_multiplier=-1).then_inc(filled, 1)
            for d in range(-3, 4):
                hold(pool, filled, 8 + d + 3)
                nc.gpsimd.affine_select(out=mem.quad_mean[:], in_=mem.quad_mean[:], compare_op=ALU.not_equal,
                                        fill=1.0 / (B * P), base=S * d, pattern=[[-1, P]],
                                        channel_multiplier=1).then_inc(filled, 1)


def column_norms(nc, mem, sems, base):
    squares_ready, squares_used, norms_summed = sems

    def act_part(act, source_ready, ready_at, norms_ready):
        for c in range(4):
            act.wait_ge(source_ready, ready_at[c // 2])
            if c >= 2:
                act.wait_ge(norms_summed, base * 4 + c - 1)
            nc.scalar.activation(mem.product[c % 2][:, :].rearrange("p (m n) -> p m n", m=4),
                                 mem.even[:, 4 * c:4 * c + 4, :], ACT.Square).then_inc(squares_ready, 1)
            if c >= 1:
                collect(act, c - 1, norms_ready)
        collect(act, 3, norms_ready)

    def collect(act, c, norms_ready):
        act.wait_ge(norms_summed, base * 4 + c + 1)
        nc.scalar.activation(mem.weights[:, c // 2, 0, 4 * (c % 2):4 * (c % 2) + 4, :],
                             mem.dots[c % 2][:, 0:4 * S].rearrange("p (m j) -> p m j", m=4),
                             ACT.Copy).then_inc(norms_ready, 1)

    def pe_part(pe, norms_ready, ready_base):
        for c in range(4):
            hold(pe, squares_ready, base * 4 + c + 1)
            if c >= 2:
                hold(pe, norms_ready, ready_base + c - 1)
            sq = mem.product[c % 2][:, :].rearrange("p (mj r) -> p mj r", r=S)
            for r in range(S):
                last = nc.tensor.matmul(mem.dots[c % 2][:, 0:4 * S], mem.ident[:], sq[:, :, r],
                                        start=(r == 0), stop=(r == S - 1))
            last.then_inc(norms_summed, 1)

    return act_part, pe_part


def normalise(nc, mem, x_dram):
    with ExitStack() as ctx:
        def sem(name):
            return ctx.enter_context(nc.semaphore(name))

        loaded, step, act_done, pe_done = sem("x_loaded"), sem("prep_step"), sem("prep_act"), sem("prep_pe")
        squared, refined = sem("prep_squared"), sem("prep_refined")
        norm_sems = (sem("prep_squares"), None, sem("prep_norms"))
        norms_ready = sem("prep_norms_ready")
        sums = ctx.enter_context(nc.sbuf_tensor("sums", [P, 4, B], F32))
        ps = mem.dots[0]
        block = ctx.enter_context(nc.Block())
        tr = "p m (c r) -> p m r c"

        @block.sync
        def _(sp):
            sp.dma_start(mem.odd[:], x_dram).then_inc(loaded, 16)

        @block.tensor
        def _(pe):
            hold(pe, step, 1)
            nc.tensor.matmul(ps[:, 0:B], mem.group[:], sums[:, 0, :], start=True, stop=True).then_inc(pe_done, 1)
            pe.wait_ge(squared, B)
            nc.tensor.matmul(ps[:, B:2 * B], mem.group[:], sums[:, 1, :], start=True, stop=True).then_inc(pe_done, 1)
            column_norms(nc, mem, norm_sems, 0)[1](pe, norms_ready, 0)
            column_norms(nc, mem, norm_sems, 1)[1](pe, norms_ready, 4)

        @block.scalar
        def _(act):
            act.wait_ge(step, 2)
            scratch = mem.work[:].rearrange("p s (m n) -> p (s m) n", n=N)
            for m in range(B):
                if m >= 12:
                    act.wait_ge(squared, m - 11)
                nc.scalar.activation(scratch[:, m % 12, :], mem.even[:, m, :], ACT.Square,
                                     accum_out=sums[:, 1, m:m + 1]).then_inc(squared, 1)
            act.wait_ge(pe_done, 2)
            nc.scalar.activation(sums[:, 2, :], ps[:, B:2 * B], ACT.Sqrt, bias=mem.eps_gn[:]).then_inc(act_done, 1)
            column_norms(nc, mem, norm_sems, 0)[0](act, step, (6, 6), norms_ready)
            act.wait_ge(step, 7)
            nc.scalar.activation(sums[:, 3, :], sums[:, 2, :], ACT.Sqrt, bias=mem.tiny[:]).then_inc(act_done, 1)
            column_norms(nc, mem, norm_sems, 1)[0](act, step, (9, 9), norms_ready)

        @block.vector
        def _(dve):
            dve.wait_ge(loaded, 16)
            nc.vector.tensor_reduce(sums[:, 0, :], mem.odd[:], AX.X, ALU.add).then_inc(step, 1)
            dve.wait_ge(pe_done, 1)
            nc.vector.tensor_tensor(mem.even[:], mem.odd[:],
                                    ps[:, 0:B].rearrange("p (m n) -> p m n", n=1).broadcast_to([P, B, N]),
                                    ALU.subtract).then_inc(step, 1)
            dve.wait_ge(step, 2)
            nc.vector.tensor_tensor(mem.odd[:].rearrange("p m (r c) -> p m r c", r=S),
                                    mem.even[:].rearrange("p m (r c) -> p m r c", r=S),
                                    mem.even[:].rearrange(tr, c=S), ALU.add).then_inc(step, 1)
            dve.wait_ge(act_done, 1)
            nc.vector.tensor_scalar(sums[:, 0, :], ps[:, B:2 * B], EPS_GN, None, ALU.add).then_inc(refined, 1)
            dve.wait_ge(refined, 1)
            refine_root(nc, dve, refined, 1, sums[:, 2, :], sums[:, 0, :], sums[:, 1, :])
            nc.vector.reciprocal(sums[:, 0, :], sums[:, 2, :]).then_inc(step, 1)
            dve.wait_ge(step, 4)
            nc.vector.tensor_scalar(sums[:, 1, :], sums[:, 0, :], 0.5, None, ALU.mult).then_inc(step, 1)
            dve.wait_ge(step, 5)
            nc.vector.tensor_tensor(mem.even[:], mem.odd[:],
                                    sums[:, 1, :].rearrange("p (m n) -> p m n", n=1).broadcast_to([P, B, N]),
                                    ALU.mult).then_inc(step, 1)
            dve.wait_ge(norms_ready, 4)
            for h in range(2):
                last = nc.vector.tensor_reduce(sums[:, 2, HB * h:HB * h + HB], mem.weights[:, h, 0], AX.X, ALU.add)
            last.then_inc(step, 1)
            dve.wait_ge(act_done, 2)
            nc.vector.tensor_scalar(mem.shift[:], sums[:, 3, :], 1.1, 1e-4, ALU.mult, ALU.add).then_inc(step, 1)
            dve.wait_ge(step, 8)
            diag = mem.even[:, :, 0:N:S + 1]
            nc.vector.tensor_tensor(diag, diag, mem.shift[:].rearrange("p (m n) -> p m n", n=1).broadcast_to([P, B, S]),
                                    ALU.add).then_inc(step, 1)


def jacobi(nc, mem):
    with ExitStack() as ctx:
        def sem(name):
            return ctx.enter_context(nc.semaphore(name))

        def small(name, *shape):
            return ctx.enter_context(nc.sbuf_tensor(name, [P, 2] + list(shape), F32))

        twice_dot = small("twice_dot", HB, PAIRS)
        weighed = small("weighed", HB, 2, PAIRS)
        cross = small("cross", HB, PAIRS)
        gap = small("gap", HB, PAIRS)
        radicand = small("radicand", HB, PAIRS)
        root = small("root", HB, PAIRS)
        gap_abs = small("gap_abs", HB, PAIRS)
        gap_sign = small("gap_sign", 2, HB, PAIRS)
        inverse = small("inverse", HB, PAIRS)
        ratio = small("ratio", 2, HB, PAIRS)
        coef = small("coef", HB, 2, PAIRS)
        secant = small("secant", HB, PAIRS)
        cosine = small("cosine", HB, PAIRS)
        moved = small("moved", 2, HB, S)
        scale = small("scale", HB, S)

        prod_ready = [sem(f"prod_ready{h}") for h in range(2)]
        dots_done = [sem(f"dots_done{h}") for h in range(2)]
        dot_read = [sem(f"dot_read{h}") for h in range(2)]
        cross_ready = [sem(f"cross_ready{h}") for h in range(2)]
        gap_ready = [sem(f"gap_ready{h}") for h in range(2)]
        root_ready = [sem(f"root_ready{h}") for h in range(2)]
        sum_ready = [sem(f"sum_ready{h}") for h in range(2)]
        inverse_ready = [sem(f"inverse_ready{h}") for h in range(2)]
        act_step = sem("act_step")
        coef_ready = [sem(f"coef_ready{h}") for h in range(2)]
        sec_ready = [sem(f"sec_ready{h}") for h in range(2)]
        cos_ready = [sem(f"cos_ready{h}") for h in range(2)]
        moved_ready = [sem(f"moved_ready{h}") for h in range(2)]
        weights_ready = [sem(f"weights_ready{h}") for h in range(2)]
        ones_ready = sem("ones_ready")
        left_over = sem("left_over")
        scale_log = sem("scale_log")
        scale_ready = sem("scale_ready")
        scaled = sem("scaled")
        norms_ready = sem("norms_ready")
        norm_sems = (sem("squares_ready"), None, sem("norms_summed"))
        dve_step, pool_step = sem("dve_step"), sem("pool_step")
        DVE_STEPS, POOL_STEPS, ACT_STEPS = 8, 22, 6

        def columns(buf, h):
            return buf[:, HB * h:HB * h + HB, :].rearrange("p m (j r) -> p m j r", r=S)

        def paired(buf, h):
            return buf[:, HB * h:HB * h + HB, :].rearrange("p m (s j r) -> p m s j r", s=2, r=S)

        def swapped(t):
            return t[:, :, ::-1]

        def over_sides(t):
            return t.rearrange("p m (s j) -> p m s j", s=1).broadcast_to([P, HB, 2, PAIRS])

        def twice(t):
            return t.rearrange("p m (s j) -> p s m j", s=1).broadcast_to([P, 2, HB, PAIRS])

        def places(src, dst):
            inner = dst[:, :, 2:S - 2]
            return [(inner, src[:, :, :, 1:PAIRS - 1]), (dst[:, :, 0:2], src[:, :, :, 0]),
                    (dst[:, :, S - 1:S - 3:-1], src[:, :, :, PAIRS - 1])]

        block = ctx.enter_context(nc.Block())

        @block.vector
        def _(dve):
            def products(h, buf):
                g = paired(buf, h)
                nc.vector.tensor_tensor(mem.product[h][:, :].rearrange("p (m j r) -> p m j r", m=HB, r=S),
                                        g[:, :, 0], g[:, :, 1], ALU.mult).then_inc(prod_ready[h], 1)

            def round_(k, src, dst, last=False):
                step = Count(dve_step, k * DVE_STEPS)
                for h in range(2):
                    part = (mem.work[:, 0:2] if h == 0 else mem.work[:, 2:0:-1])
                    part = part.rearrange("p s (m j r) -> p m s j r", m=HB, r=S)
                    dve.wait_ge(coef_ready[h], k + 1)
                    cb = coef[:, h].rearrange("p m s (j r) -> p m s j r", r=1).broadcast_to([P, HB, 2, PAIRS, S])
                    chained(dve, step, nc.vector.tensor_tensor(part, swapped(paired(src, h)), cb, ALU.mult))
                    g, d = paired(src, h), columns(dst, h)
                    for n, ((to, a), (_, b)) in enumerate(zip(places(g, d), places(part, d))):
                        if n == 0:
                            to = to.rearrange("p m (s j) r -> p m s j r", s=2)
                        ins = nc.vector.tensor_tensor(to, a, b, ALU.add)
                        if n < 2:
                            step.up(ins)
                        else:
                            chained(dve, step, ins)
                    if not last:
                        products(h, dst)

            with dve.Fori(0, SWEEPS) as sw:
                k0 = sw * ROUNDS
                for h in range(2):
                    products(h, mem.even)
                with dve.Fori(0, ROUNDS // 2) as i:
                    round_(k0 + i * 2, mem.even, mem.odd)
                    round_(k0 + i * 2 + 1, mem.odd, mem.even)
                round_(k0 + ROUNDS - 1, mem.even, mem.odd, last=True)
                w = mem.weights
                for h in range(2):
                    dve.wait_ge(scale_ready, sw * 2 + h + 1)
                    for n, ins in enumerate((lambda: nc.vector.tensor_tensor(moved[:, h, 0], scale[:, h], scale[:, h], ALU.mult),
                                             lambda: nc.vector.reciprocal(moved[:, h, 0], moved[:, h, 0]),
                                             lambda: nc.vector.tensor_tensor(w[:, h, 1], w[:, h, 1], moved[:, h, 0], ALU.mult))):
                        ins().then_inc(left_over, 1)
                        dve.wait_ge(left_over, sw * 6 + h * 3 + n + 1)
                    sb = scale[:, h].rearrange("p m (j r) -> p m j r", r=1).broadcast_to([P, HB, S, S])
                    nc.vector.tensor_tensor(columns(mem.even, h), columns(mem.odd, h), sb, ALU.mult).then_inc(scaled, 1)
                dve.wait_ge(scaled, sw * 2 + 2)
                dve.wait_ge(norms_ready, sw * 4 + 4)

        @block.tensor
        def _(pe):
            def round_(k):
                for h in range(2):
                    hold(pe, prod_ready[h], k + 1)
                    pr = mem.product[h][:, :].rearrange("p (mj r) -> p mj r", r=S)
                    for r in range(S):
                        last = nc.tensor.matmul(mem.dots[h][:, 0:P], mem.ident[:], pr[:, :, r],
                                                start=(r == 0), stop=(r == S - 1))
                    last.then_inc(dots_done[h], 1)

            with pe.Fori(0, SWEEPS) as sw:
                with pe.Fori(0, ROUNDS) as i:
                    round_(sw * ROUNDS + i)
                column_norms(nc, mem, norm_sems, sw)[1](pe, norms_ready, sw * 4)

        @block.scalar
        def _(act):
            def round_(k):
                step = Count(act_step, k * ACT_STEPS)
                for h in range(2):
                    act.wait_ge(gap_ready[h], k + 1)
                    nc.scalar.activation(gap_abs[:, h], gap[:, h], ACT.Abs)
                    nc.scalar.activation(gap_sign[:, h, 1], gap[:, h], ACT.Sign, bias=mem.tiny[:])
                    nc.scalar.activation(gap_sign[:, h, 0], gap[:, h], ACT.Sign, scale=-1.0, bias=mem.minus_tiny[:])
                    act.wait_ge(dots_done[h], k + 1)
                    nc.scalar.activation(twice_dot[:, h].rearrange("p m j -> p (m j)"), mem.dots[h][:, 0:P], ACT.Copy,
                                         scale=2.0).then_inc(dot_read[h], 1)
                    act.wait_ge(cross_ready[h], k + 1)
                    chained(act, step, nc.scalar.activation(root[:, h], radicand[:, h], ACT.Ln, bias=mem.tiny_log[:]))
                    nc.scalar.activation(root[:, h], root[:, h], ACT.Exp, scale=0.5).then_inc(root_ready[h], 1)
                    act.wait_ge(sum_ready[h], k + 1)
                    chained(act, step, nc.scalar.activation(inverse[:, h], root[:, h], ACT.Ln))
                    nc.scalar.activation(inverse[:, h], inverse[:, h], ACT.Exp, scale=-1.0).then_inc(inverse_ready[h], 1)
                    act.wait_ge(sec_ready[h], k + 1)
                    chained(act, step, nc.scalar.activation(cosine[:, h], secant[:, h], ACT.Ln))
                    nc.scalar.activation(cosine[:, h], cosine[:, h], ACT.Exp, scale=-1.0).then_inc(cos_ready[h], 1)
                    act.wait_ge(moved_ready[h], k + 1)
                    src = moved[:, h].rearrange("p k m (s j) -> p (k m) s j", s=2)
                    dst = mem.weights[:, h].rearrange("p k m c -> p (k m) c")
                    for n, (to, a) in enumerate(places(src, dst)):
                        if n == 0:
                            to = to.rearrange("p m (s j) -> p m s j", s=2)
                        last = nc.scalar.activation(to, a, ACT.Copy)
                    last.then_inc(weights_ready[h], 1)

            nc.scalar.preload_act_table_set("natural_log_exp_and_others")
            with act.Fori(0, SWEEPS) as sw:
                with act.Fori(0, ROUNDS) as i:
                    round_(sw * ROUNDS + i)
                for h in range(2):
                    act.wait_ge(weights_ready[h], (sw + 1) * ROUNDS)
                    nc.scalar.activation(scale[:, h], mem.weights[:, h, 1], ACT.Ln).then_inc(scale_log, 1)
                    act.wait_ge(scale_log, sw * 2 + h + 1)
                    nc.scalar.activation(scale[:, h], scale[:, h], ACT.Exp, scale=0.5).then_inc(scale_ready, 1)
                column_norms(nc, mem, norm_sems, sw)[0](act, scaled, (sw * 2 + 1, sw * 2 + 2), norms_ready)

        @block.gpsimd
        def _(pool):
            def round_(k):
                step = Count(pool_step, k * POOL_STEPS)
                for h in range(2):
                    w = mem.weights[:, h, 1].rearrange("p m (s j) -> p m s j", s=2)
                    norm = mem.weights[:, h, 0].rearrange("p m (s j) -> p m s j", s=2)
                    chained(pool, step, nc.gpsimd.tensor_tensor(gap[:, h], norm[:, :, 1], norm[:, :, 0], ALU.subtract))
                    nc.gpsimd.tensor_tensor(radicand[:, h], gap[:, h], gap[:, h], ALU.mult).then_inc(gap_ready[h], 1)
                    hold(pool, dot_read[h], k + 1)
                    chained(pool, step, nc.gpsimd.tensor_tensor(weighed[:, h], swapped(w), over_sides(twice_dot[:, h]),
                                                                ALU.mult))
                    chained(pool, step, nc.gpsimd.tensor_tensor(cross[:, h], weighed[:, h, :, 0], weighed[:, h, :, 1],
                                                                ALU.mult))
                    nc.gpsimd.tensor_tensor(radicand[:, h], radicand[:, h], cross[:, h], ALU.add).then_inc(cross_ready[h], 1)
                    hold(pool, root_ready[h], k + 1)
                    nc.gpsimd.tensor_tensor(root[:, h], root[:, h], gap_abs[:, h], ALU.add).then_inc(sum_ready[h], 1)
                    hold(pool, inverse_ready[h], k + 1)
                    chained(pool, step, nc.gpsimd.tensor_tensor(ratio[:, h], twice(inverse[:, h]), gap_sign[:, h], ALU.mult))
                    by_pair = ratio[:, h].rearrange("p s m j -> p m s j")
                    nc.gpsimd.tensor_tensor(coef[:, h], weighed[:, h], by_pair, ALU.mult).then_inc(coef_ready[h], 1)
                    hold(pool, coef_ready[h], k + 1)
                    chained(pool, step, nc.gpsimd.tensor_tensor(secant[:, h], coef[:, h, :, 0], coef[:, h, :, 1], ALU.mult))
                    nc.gpsimd.tensor_tensor(secant[:, h], mem.one[:], secant[:, h], ALU.subtract).then_inc(sec_ready[h], 1)
                    mv = moved[:, h].rearrange("p k m (s j) -> p k m s j", s=2)
                    chained(pool, step, nc.gpsimd.tensor_tensor(cross[:, h], cross[:, h], mem.half[:], ALU.mult))
                    chained(pool, step, nc.gpsimd.tensor_tensor(mv[:, 0], over_sides(cross[:, h]), by_pair, ALU.mult))
                    step.up(nc.gpsimd.tensor_tensor(mv[:, 0], mv[:, 0], norm, ALU.add))
                    hold(pool, cos_ready[h], k + 1)
                    chained(pool, step, nc.gpsimd.tensor_tensor(secant[:, h], secant[:, h], cosine[:, h], ALU.mult))
                    chained(pool, step, nc.gpsimd.tensor_tensor(secant[:, h], mem.two[:], secant[:, h], ALU.subtract))
                    chained(pool, step, nc.gpsimd.tensor_tensor(cosine[:, h], cosine[:, h], secant[:, h], ALU.mult))
                    nc.gpsimd.tensor_tensor(mv[:, 1], w, over_sides(cosine[:, h]), ALU.mult).then_inc(moved_ready[h], 1)
                    hold(pool, weights_ready[h], k + 1)

            for h in range(2):
                nc.gpsimd.memset(mem.weights[:, h, 1], 1.0).then_inc(ones_ready, 1)
            pool.wait_ge(ones_ready, 2)
            with pool.Fori(0, SWEEPS) as sw:
                with pool.Fori(0, ROUNDS) as i:
                    round_(sw * ROUNDS + i)
                hold(pool, left_over, sw * 6 + 6)
                hold(pool, norms_ready, sw * 4 + 4)


def logarithm(nc, mem):
    with ExitStack() as ctx:
        def sem(name):
            return ctx.enter_context(nc.semaphore(name))

        def per_column(name):
            return ctx.enter_context(nc.sbuf_tensor(name, [P, 2, HB, S], F32))

        true_square, true_length, hat_length = (per_column(n) for n in ("true_square", "true_length", "hat_length"))
        height, root_height, spare = (per_column(n) for n in ("height", "root_height", "log_spare"))
        factor = ctx.enter_context(nc.sbuf_tensor("factor", [P, B, S], F32))
        banks = mem.banks
        spectrum, step = sem("spectrum"), sem("log_step")
        staged, turned, turned_out, formed = (sem(n) for n in ("log_staged", "log_turned", "log_turned_out", "log_formed"))
        formed_out = (sem("log_out_by_act"), sem("log_out_by_dve"))
        summed, averaged = sem("log_summed"), sem("log_averaged")
        stage = mem.product[0].rearrange("p (r q j) -> p r q j", q=4, j=S)
        tcol = mem.work[:, 1].rearrange("p (k r) -> p k r", r=S)
        logs = mem.odd[:].rearrange("p (a b) n -> p a (b n)", a=QUADS)
        hat_square, left_over = mem.weights[:, :, 0], mem.weights[:, :, 1]
        fac2 = factor[:].rearrange("p (h m) c -> p h m c", h=2)
        block = ctx.enter_context(nc.Block())

        @block.scalar
        def _(act):
            nc.scalar.activation(hat_length[:], hat_square, ACT.Sqrt)
            act.wait_ge(step, 1)
            nc.scalar.activation(true_length[:], true_square[:], ACT.Sqrt).then_inc(spectrum, 1)
            act.wait_ge(step, 11)
            nc.scalar.activation(height[:], true_length[:], ACT.Ln).then_inc(spectrum, 1)
            act.wait_ge(step, 13)
            nc.scalar.activation(root_height[:], height[:], ACT.Sqrt, bias=mem.tiny[:]).then_inc(spectrum, 1)
            with act.Fori(0, QUADS) as g:
                for b in range(8):
                    act.wait_ge(turned, g * 8 + b + 1)
                    nc.scalar.activation(tcol[:, :, 4 * b:4 * b + 4],
                                         banks[b % 4][:].rearrange("p (r k) -> p k r", r=4), ACT.Copy).then_inc(turned_out, 1)
                for b in range(0, 8, 2):
                    act.wait_ge(formed, g * 8 + b + 1)
                    nc.scalar.activation(logs[:, g, 512 * b:512 * b + 512], banks[4 + b % 4][:], ACT.Copy)\
                        .then_inc(formed_out[0], 1)

        @block.vector
        def _(dve):
            nc.vector.tensor_tensor(true_square[:], hat_square, left_over, ALU.mult).then_inc(step, 1)
            dve.wait_ge(spectrum, 1)
            refine_root(nc, dve, step, 1, hat_length[:], hat_square, spare[:])
            refine_root(nc, dve, step, 5, true_length[:], true_square[:], spare[:])
            sh = mem.shift[:].rearrange("p (h m n) -> p h m n", h=2, n=1).broadcast_to([P, 2, HB, S])
            nc.vector.tensor_tensor(true_length[:], true_length[:], sh, ALU.subtract).then_inc(step, 1)
            dve.wait_ge(step, 10)
            nc.vector.tensor_scalar(true_length[:], true_length[:], EPS_LOG, None, ALU.max).then_inc(step, 1)
            dve.wait_ge(spectrum, 2)
            nc.vector.tensor_scalar(height[:], height[:], -math.log(EPS_LOG), 0.0, ALU.add, ALU.max).then_inc(step, 1)
            nc.vector.reciprocal(hat_length[:], hat_length[:]).then_inc(step, 1)
            dve.wait_ge(spectrum, 3)
            refine_root(nc, dve, step, 13, root_height[:], height[:], spare[:])
            nc.vector.tensor_tensor(fac2, root_height[:], hat_length[:], ALU.mult).then_inc(step, 1)
            dve.wait_ge(step, 18)
            with dve.Fori(0, QUADS) as g:
                fb = factor[:, bass.ds(g * 4, 4), :].rearrange("p q (j r) -> p q j r", r=1).broadcast_to([P, 4, S, S])
                src = mem.even[:, bass.ds(g * 4, 4), :].rearrange("p q (j r) -> p q j r", r=S)
                nc.vector.tensor_tensor(stage.rearrange("p r q j -> p q j r"), src, fb, ALU.mult).then_inc(staged, 1)
                for b in range(1, 8, 2):
                    dve.wait_ge(formed, g * 8 + b + 1)
                    nc.vector.tensor_copy(logs[:, g, 512 * b:512 * b + 512], banks[4 + b % 4][:]).then_inc(formed_out[1], 1)
            for out in formed_out:
                dve.wait_ge(out, QUADS * 4)
            nc.vector.tensor_reduce(factor[:, 0, :], mem.odd[:].rearrange("p a (b n) -> p n (a b)", n=S), AX.X,
                                    ALU.add).then_inc(summed, 1)

        @block.tensor
        def _(pe):
            with pe.Fori(0, QUADS) as g:
                hold(pe, staged, g + 1)
                for b in range(8):
                    if b >= 4:
                        hold(pe, turned_out, g * 8 + b - 3)
                    for r in range(4):
                        last = nc.tensor.matmul(banks[b % 4][:, P * r:P * r + P],
                                                stage[:, 4 * b + r].rearrange("p q j -> p (q j)"), mem.ident[:],
                                                start=True, stop=True)
                    last.then_inc(turned, 1)
                hold(pe, turned_out, g * 8 + 8)
                for b in range(8):
                    if b >= 4:
                        hold(pe, formed_out[b % 2], g * 4 + (b - 4) // 2 + 1)
                    quad_products(nc, banks[4 + b % 4], tcol, tcol, 16 * b).then_inc(formed, 1)
                for out in formed_out:
                    hold(pe, out, g * 4 + 4)
            hold(pe, summed, 1)
            nc.tensor.matmul(banks[0][:, 0:S], mem.quad_mean[:], factor[:, 0, :], start=True, stop=True)\
                .then_inc(averaged, 1)

        @block.gpsimd
        def _(pool):
            hold(pool, averaged, 1)


def quad_products(nc, bank, left, right, first):
    for k in range(16):
        for q in range(4):
            rows = slice(S * q, S * q + S)
            last = nc.tensor.matmul(bank[rows, S * k:S * k + S], left[rows, first + k, :], right[rows, first + k, :],
                                    start=True, stop=True)
    return last


def exponential(nc, mem, gamma_dram, beta_dram):
    TM = 32
    W = TM * S
    TILES = B * N // W
    STEPS = 3 + SQUARINGS
    with ExitStack() as ctx:
        def sem(name):
            return ctx.enter_context(nc.semaphore(name))

        def tile(name):
            return ctx.enter_context(nc.sbuf_tensor(name, [P, TM, S], F32))

        a1, a2, a3, low, high = (tile(n) for n in ("a1", "a2", "a3", "low", "high"))
        power = [tile("power0"), tile("power1")]
        scal = ctx.enter_context(nc.sbuf_tensor("scal", [P, 4], F32))
        offset = ctx.enter_context(nc.sbuf_tensor("offset", [P, S], F32))
        eye = ctx.enter_context(nc.sbuf_tensor("eye", [P, 2, S], F32))
        loaded, step, eyes = sem("gb_loaded"), sem("exp_step"), sem("eyes")
        a_ready, product_done = sem("a_ready"), sem("product_done")
        copied = sem("copied")
        high_ready, low_ready = sem("high_ready"), sem("low_ready")
        banks = mem.banks
        logs = mem.odd[:].rearrange("p m n -> p (m n)")
        block = ctx.enter_context(nc.Block())
        c = TAYLOR

        def over(t):
            return t.rearrange("p (k c) -> p k c", k=1).broadcast_to([P, TM, S])

        @block.sync
        def _(sp):
            sp.dma_start(scal[:, 0:1], gamma_dram.partition_broadcast(P)).then_inc(loaded, 16)
            sp.dma_start(scal[:, 1:2], beta_dram.partition_broadcast(P)).then_inc(loaded, 16)

        @block.gpsimd
        def _(pool):
            for n, v in enumerate((c[0], c[3])):
                nc.gpsimd.memset(eye[:, n], 0.0).then_inc(eyes, 1)
            hold(pool, eyes, 2)
            n = 2
            for k, v in enumerate((c[0], c[3])):
                for q in range(4):
                    nc.gpsimd.affine_select(out=eye[:, k], in_=eye[:, k], compare_op=ALU.not_equal, fill=v,
                                            base=-S * q, pattern=[[-1, S]], channel_multiplier=1).then_inc(eyes, 1)
                    n += 1
                    hold(pool, eyes, n)

        @block.vector
        def _(dve):
            dve.wait_ge(loaded, 32)
            shrink = 2.0 ** -SQUARINGS
            nc.vector.tensor_scalar(scal[:, 2:3], scal[:, 0:1], -shrink, None, ALU.mult).then_inc(step, 1)
            nc.vector.tensor_scalar(scal[:, 3:4], scal[:, 1:2], shrink, None, ALU.mult).then_inc(step, 1)
            nc.vector.tensor_scalar(scal[:, 0:1], scal[:, 0:1], shrink, None, ALU.mult).then_inc(step, 1)
            dve.wait_ge(step, 3)
            nc.vector.tensor_scalar(offset[:], mem.banks[0][:, 0:S], scal[:, 2:3], scal[:, 3:4], ALU.mult, ALU.add)\
                .then_inc(step, 1)
            dve.wait_ge(step, 4)
            dve.wait_ge(eyes, 10)
            with dve.Fori(0, TILES) as t:
                k = Count(step, t * 2 + 4)
                nc.vector.scalar_tensor_tensor(a1[:], logs[:, bass.ds(t * W, W)].rearrange("p (k c) -> p k c", c=S),
                                               scal[:, 0:1], over(offset[:]), ALU.mult, ALU.add).then_inc(a_ready, 1)
                dve.wait_ge(a_ready, t + 1)
                nc.vector.scalar_tensor_tensor(low[:], a1[:], c[1], over(eye[:, 0]), ALU.mult, ALU.add)
                chained(dve, k, nc.vector.scalar_tensor_tensor(high[:], a1[:], c[4], over(eye[:, 1]), ALU.mult, ALU.add))
                dve.wait_ge(copied, t * (2 * STEPS) + 2)
                nc.vector.scalar_tensor_tensor(low[:], a2[:], c[2], low[:], ALU.mult, ALU.add)
                chained(dve, k, nc.vector.scalar_tensor_tensor(high[:], a2[:], c[5], high[:], ALU.mult, ALU.add))
                dve.wait_ge(copied, t * (2 * STEPS) + 4)
                nc.vector.scalar_tensor_tensor(high[:], a3[:], c[6], high[:], ALU.mult, ALU.add).then_inc(high_ready, 1)
                for g in range(2):
                    dve.wait_ge(product_done, t * (2 * STEPS) + 5 + g)
                    nc.vector.tensor_tensor(power[0][:, 16 * g:16 * g + 16, :],
                                            banks[4 + g][:].rearrange("p (k c) -> p k c", c=S),
                                            low[:, 16 * g:16 * g + 16, :], ALU.add).then_inc(low_ready, 1)

        @block.scalar
        def _(act):
            with act.Fori(0, TILES) as t:
                for n in range(STEPS):
                    if n == 2:
                        continue
                    dest = a2 if n == 0 else a3 if n == 1 else power[n % 2]
                    for g in range(2):
                        act.wait_ge(product_done, t * (2 * STEPS) + 2 * n + g + 1)
                        src = banks[2 * (n % 4) + g][:]
                        if n < STEPS - 1:
                            out = dest[:, 16 * g:16 * g + 16, :].rearrange("p k c -> p (k c)")
                        else:
                            out = logs[:, bass.ds(t * W + 512 * g, 512)]
                        nc.scalar.activation(out, src, ACT.Copy).then_inc(copied, 1 if n != 1 or g == 0 else 1)
                    if n == 1:
                        act.wait_ge(low_ready, t * 2 + 2)
                        for g in range(2):
                            nc.scalar.sem_inc(copied, 1)

        @block.tensor
        def _(pe):
            with pe.Fori(0, TILES) as t:
                for n in range(STEPS):
                    left, right = {0: (a1, a1), 1: (a1, a2), 2: (a3, high)}.get(n, (power[(n - 1) % 2],) * 2)
                    for g in range(2):
                        if n == 0:
                            hold(pe, a_ready, t + 1)
                        elif n == 2:
                            hold(pe, high_ready, t + 1)
                        else:
                            hold(pe, copied, t * (2 * STEPS) + 2 * (n - 1) + g + 1)
                        quad_products(nc, banks[2 * (n % 4) + g], left, right, 16 * g).then_inc(product_done, 1)


def back_to_channels(nc, mem, x_dram):
    with ExitStack() as ctx:
        def sem(name):
            return ctx.enter_context(nc.semaphore(name))

        loaded, staged, turned, added = sem("x_again"), sem("back_staged"), sem("back_turned"), sem("back_added")
        stage = [mem.work[:, n].rearrange("p (c k) -> p c k", k=P) for n in range(2)]
        powers = mem.odd[:].rearrange("p (g b) n -> p g (b n)", g=QUADS)
        banks = mem.banks
        block = ctx.enter_context(nc.Block())

        @block.sync
        def _(sp):
            sp.dma_start(mem.even[:], x_dram).then_inc(loaded, 16)

        @block.gpsimd
        def _(pool):
            hold(pool, loaded, 16)

        @block.scalar
        def _(act):
            with act.Fori(0, QUADS) as g:
                nc.scalar.activation(stage[0].rearrange("p c k -> p k c"),
                                     powers[:, g, :].rearrange("p (k c) -> p k c", c=S), ACT.Copy).then_inc(staged, 1)
                act.wait_ge(turned, g * 8 + 8)

        @block.tensor
        def _(pe):
            with pe.Fori(0, QUADS) as g:
                hold(pe, staged, g + 1)
                for b in range(8):
                    if b >= 4:
                        hold(pe, added, g * 8 + b - 3)
                    for n in range(4):
                        last = nc.tensor.matmul(banks[b % 4][:, P * n:P * n + P], stage[0][:, 4 * b + n, :], mem.ident[:],
                                                start=True, stop=True)
                    last.then_inc(turned, 1)
                hold(pe, added, g * 8 + 8)

        @block.vector
        def _(dve):
            dve.wait_ge(loaded, 16)
            with dve.Fori(0, QUADS) as g:
                for b in range(8):
                    dve.wait_ge(turned, g * 8 + b + 1)
                    d = mem.even[:, bass.ds(g * 4, 4), :].rearrange("p q (r c) -> p q r c", c=S)[:, :, :, 4 * b:4 * b + 4]
                    d = d.rearrange("p q r c -> p c q r")
                    nc.vector.tensor_tensor(d, d, banks[b % 4][:].rearrange("p (c q r) -> p c q r", c=4, q=4),
                                            ALU.add).then_inc(added, 1)


HEADS = 8
DH = P // HEADS
SLOT = 32
GROUPS = 2
QB = N // 2
KT = N // P
TOPK = 32
EXPERTS = 4
RANK = 16
LORA = EXPERTS * RANK
EPS_LN = 1e-5
OCTANTS = 8
MARGIN = 24.0
NEGATIVE = -3.0e38
UNITS = 2 * GROUPS


class Tiles:

    def __init__(self, sb):
        self.wq = sb("w_wq", [P, GROUPS, P])
        self.wk = sb("w_wk", [P, GROUPS, P])
        self.wv = sb("w_wv", [P, P])
        self.wo = sb("w_wo", [P, GROUPS, P])
        self.bo = sb("w_bo", [P, 1])
        self.fc1t = sb("w_fc1t", [P, EXPERTS, P])
        self.lora_a = sb("w_lora_a", [P, EXPERTS, LORA])
        self.lora_out = sb("w_lora_out", [LORA, P])
        self.gates_t = sb("w_gates_t", [P, EXPERTS + 1])
        self.average = sb("w_average", [P, P])
        self.mean_column = sb("w_mean_column", [P, 1])
        self.select = sb("w_select", [P, P])
        self.row16 = sb("w_row16", [P, 1])
        self.spread = sb("w_spread", [P, 4, P])
        self.centred = sb("w_centred", [P, N])
        self.squares = sb("w_squares", [P, N])
        self.z = sb("w_z", [P, N])
        self.t = sb("w_t", [P, N])
        self.var = sb("w_var", [P, KT])
        self.var_spare = sb("w_var_spare", [P, KT])
        self.root = sb("w_root", [P, KT])
        self.root_wide = sb("w_root_wide", [P, KT, P])
        self.q = sb("w_q", [P, GROUPS, N])
        self.k = sb("w_k", [P, GROUPS, N])
        self.q_shifted = sb("w_q_shifted", [P, GROUPS, N])
        self.v = sb("w_v", [P, KT, HEADS, SLOT])
        self.best = sb("w_best", [P, 16, OCTANTS, 8])
        self.top = sb("w_top", [P, 16])
        self.eighth = sb("w_eighth", [P, 16])
        self.widest = sb("w_widest", [P, 2, 16])
        self.o = sb("w_o", [P, QB])
        self.inverse = sb("w_inverse", [P, QB])
        self.att = sb("w_att", [P, GROUPS, N])
        self.hid = sb("w_hid", [P, 2 * EXPERTS, QB])
        self.low = sb("w_low", [LORA, 2, QB])
        self.gate = sb("w_gate", [P, KT, EXPERTS])
        self.threshold = sb("w_threshold", [P, KT])
        self.gate_sum = sb("w_gate_sum", [P, KT])
        self.gate_wide = sb("w_gate_wide", [P, KT, LORA])
        self.scores = sb("w_scores", [P, N])
        self.rest = sb("w_rest", [P, N])
        self.masked = sb("w_masked", [P, N])
        self.turned = sb("w_turned", [P, KT, P])
        self.eight = sb("w_eight", [P, TOPK // 8, 8])
        self.minus_top = sb("w_minus_top", [P, 1])
        self.exp = [sb(f"w_exp{n}", [P, QB]) for n in range(4)]


def load_weights(nc, mem, w, dram):
    with ExitStack() as ctx:
        def sem(name):
            return ctx.enter_context(nc.semaphore(name))

        def sb(name, shape):
            return ctx.enter_context(nc.sbuf_tensor(name, shape, F32))

        cleared, loaded, turned, copied, selected = (sem(n) for n in ("w_cleared", "w_loaded", "w_turned", "w_copied",
                                                                      "w_selected"))
        fc1, fc2 = sb("fc1", [P, EXPERTS, P]), sb("fc2", [P, EXPERTS, P])
        gates = sb("gates", [EXPERTS + 1, P])
        lora_b = sb("lora_b", [RANK, EXPERTS, P])
        fc2t = sb("fc2t", [P, EXPERTS, P])
        lora_bt = sb("lora_bt", [P, EXPERTS, LORA])
        banks = mem.banks
        DMAS = 2 + 1 + 8 + 1 + 1 + 1 + 1 + 1 + 4 + 1
        block = ctx.enter_context(nc.Block())
        pads = (w.wq, w.wk, w.wo, w.lora_a, lora_bt, w.select, w.spread)

        @block.gpsimd
        def _(pool):
            for t in pads:
                nc.gpsimd.memset(t[:], 0.0).then_inc(cleared, 1)
            nc.gpsimd.memset(w.average[:], 1.0 / P)
            nc.gpsimd.memset(w.mean_column[:], 1.0 / P)
            nc.gpsimd.memset(w.v[:], 1.0)
            nc.gpsimd.memset(w.row16[:], 0.0).then_inc(cleared, 1)
            nc.gpsimd.memset(w.widest[:], 0.0).then_inc(cleared, 1)
            pool.wait_ge(cleared, len(pads) + 2)
            nc.gpsimd.affine_select(out=w.select[:].rearrange("p (j r) -> p j r", r=SLOT),
                                    in_=w.select[:].rearrange("p (j r) -> p j r", r=SLOT),
                                    compare_op=ALU.not_equal, fill=1.0, base=-DH, pattern=[[-SLOT, 4], [0, SLOT]],
                                    channel_multiplier=1).then_inc(selected, 1)
            for j in range(4):
                nc.gpsimd.affine_select(out=w.row16[:], in_=w.row16[:], compare_op=ALU.not_equal, fill=1.0,
                                        base=-DH - SLOT * j, pattern=[[0, 1]], channel_multiplier=1).then_inc(selected, 1)
                pool.wait_ge(selected, j + 2)

        @block.sync
        def _(sp):
            sp.wait_ge(cleared, len(pads) + 2)

            def load(out, in_):
                sp.dma_start(out, in_).then_inc(loaded, 16)

            for pad, name in ((w.wq, "wq"), (w.wk, "wk")):
                load(pad[:].rearrange("c g (j r) -> c (g j) r", r=SLOT)[:, :, 0:DH],
                     dram[name].rearrange("c (h d) -> c h d", d=DH))
            load(w.wv[:], dram["wv"])
            for h in range(HEADS):
                j = h % 4
                load(w.wo[SLOT * j:SLOT * j + DH, h // 4, :], dram["wo"][DH * h:DH * h + DH, :])
            load(w.bo[:], dram["bo"].rearrange("(c n) -> c n", n=1))
            load(fc1[:], dram["fc1"].rearrange("e h i -> h e i"))
            load(fc2[:], dram["fc2"].rearrange("e d o -> d e o"))
            load(gates[0:EXPERTS, :], dram["gate"])
            load(gates[EXPERTS:EXPERTS + 1, :], dram["thr"])
            for e in range(EXPERTS):
                load(w.lora_a[:, e, RANK * e:RANK * e + RANK], dram["lora_a"][e])
            load(lora_b[:], dram["lora_b"].rearrange("e r o -> r e o"))
            sp.wait_ge(loaded, 16 * DMAS)

        @block.tensor
        def _(pe):
            pe.wait_ge(loaded, 16 * DMAS)
            for e in range(EXPERTS):
                nc.tensor.matmul(banks[0][:, P * e:P * e + P], fc1[:, e, :], mem.ident[:], start=True, stop=True)
                nc.tensor.matmul(banks[1][:, P * e:P * e + P], fc2[:, e, :], mem.ident[:], start=True, stop=True)
                nc.tensor.matmul(banks[2][:, RANK * e:RANK * e + RANK], lora_b[:, e, :], mem.ident[0:RANK, 0:RANK],
                                 start=True, stop=True)
            nc.tensor.matmul(banks[3][:, 0:EXPERTS + 1], gates[:], mem.ident[0:EXPERTS + 1, 0:EXPERTS + 1],
                             start=True, stop=True).then_inc(turned, 1)
            pe.wait_ge(copied, 1)
            for e in range(EXPERTS):
                last = nc.tensor.matmul(banks[4][0:LORA, 0:P], lora_bt[:, e, :], fc2t[:, e, :],
                                        start=(e == 0), stop=(e == EXPERTS - 1))
            last.then_inc(turned, 1)

        @block.vector
        def _(dve):
            dve.wait_ge(turned, 1)
            nc.vector.tensor_copy(w.fc1t[:].rearrange("p e n -> p (e n)"), banks[0][:])
            nc.vector.tensor_copy(fc2t[:].rearrange("p e n -> p (e n)"), banks[1][:])
            for e in range(EXPERTS):
                nc.vector.tensor_copy(lora_bt[:, e, RANK * e:RANK * e + RANK], banks[2][:, RANK * e:RANK * e + RANK])
            nc.vector.tensor_copy(w.gates_t[:], banks[3][:, 0:EXPERTS + 1]).then_inc(copied, 1)
            dve.wait_ge(turned, 2)
            nc.vector.tensor_copy(w.lora_out[:], banks[4][0:LORA, 0:P]).then_inc(copied, 1)


class PassSemaphores:

    def __init__(self, sem):
        self.averaged = sem("averaged")
        self.centred = sem("centred")
        self.squared = sem("squared")
        self.variances = sem("variances")
        self.spread_ready = sem("spread_ready")
        self.stats = sem("stats")
        self.rooted = sem("rooted")
        self.scale_spread = sem("scale_spread")
        self.normal = sem("normal")
        self.projected = sem("projected")
        self.q_out = sem("q_out")
        self.k_out = sem("k_out")
        self.v_out = sem("v_out")
        self.scored = sem("scored")
        self.read_max = sem("read_max")
        self.max_spread = sem("max_spread")
        self.max_turned = sem("max_turned")
        self.shifted = sem("shifted")
        self.scores_t = sem("scores_t")
        self.exp_done = sem("exp_done")
        self.weighed = sem("weighed")
        self.gathered = sem("gathered")
        self.den_spread = sem("den_spread")
        self.den_inverse = sem("den_inverse")
        self.inv_step = sem("inv_step")
        self.attended = sem("attended")
        self.joined = sem("joined")
        self.residual = sem("residual")
        self.gated = sem("gated")
        self.gate_exp = sem("gate_exp")
        self.gate_done = sem("gate_done")
        self.gates_t_done = sem("gates_t_done")
        self.hidden = sem("hidden")
        self.hidden_act = sem("hidden_act")
        self.hidden_dve = sem("hidden_dve")
        self.low = sem("low")
        self.low_out = sem("low_out")
        self.mixed = sem("mixed")
        self.mixed_low = sem("mixed_low")
        self.expert_out = sem("expert_out")
        self.finished = sem("finished")
        self.stored = sem("stored")
        self.dve_stats = sem("dve_stats")
        self.gate_steps = sem("gate_steps")
        self.maxima = sem("maxima")
        self.g_copied = sem("g_copied")
        self.g_ranked = sem("g_ranked")
        self.g_exp = sem("g_exp")
        self.g_masked = sem("g_masked")
        self.g_turned = sem("g_turned")
        self.g_turned_out = sem("g_turned_out")
        self.g_pv = sem("g_pv")
        self.rank_steps = sem("rank_steps")


def image_pass(nc, mem, w, s, out_dram, general):
    banks = mem.banks
    first = B if general else 0

    def tokens(b):
        return mem.even[:, bass.ds(b - first, 1), :].rearrange("p m n -> p (m n)")

    def norm_pe(pe, n, source):
        for k in range(2):
            last = nc.tensor.matmul(banks[k][:], w.average[:], source[:, QB * k:QB * k + QB], start=True, stop=True)
        last.then_inc(s.averaged, 1)
        hold(pe, s.squared, n + 1)
        for t in range(KT):
            last = nc.tensor.matmul(banks[2][:, t:t + 1], w.squares[:, P * t:P * t + P], w.mean_column[:],
                                    start=True, stop=True)
        last.then_inc(s.variances, 1)
        hold(pe, s.spread_ready, n + 1)
        for t in range(KT):
            last = nc.tensor.matmul(banks[t // 4][:, P * (t % 4):P * (t % 4) + P],
                                    w.root_wide[:, t, :], mem.ident[:], start=True, stop=True)
        last.then_inc(s.scale_spread, 1)

    def norm_act(act, n):
        act.wait_ge(s.centred, n + 1)
        nc.scalar.activation(w.squares[:], w.centred[:], ACT.Square).then_inc(s.squared, 1)
        act.wait_ge(s.stats, n + 1)
        nc.scalar.activation(w.root[:], w.var[:], ACT.Ln).then_inc(s.rooted, 1)
        act.wait_ge(s.rooted, n * 2 + 1)
        nc.scalar.activation(w.root[:], w.root[:], ACT.Exp, scale=0.5).then_inc(s.rooted, 1)

    def norm_dve(dve, n, source, result):
        dve.wait_ge(s.averaged, n + 1)
        for k in range(2):
            last = nc.vector.tensor_tensor(w.centred[:, QB * k:QB * k + QB], source[:, QB * k:QB * k + QB], banks[k][:],
                                           ALU.subtract)
        last.then_inc(s.centred, 1)
        dve.wait_ge(s.variances, n + 1)
        nc.vector.tensor_scalar(w.var[:], banks[2][:, 0:KT], EPS_LN, None, ALU.add).then_inc(s.stats, 1)
        dve.wait_ge(s.rooted, n * 2 + 2)
        refine_root(nc, dve, s.dve_stats, n * 5, w.root[:], w.var[:], w.var_spare[:])
        nc.vector.reciprocal(w.root[:], w.root[:]).then_inc(s.dve_stats, 1)
        dve.wait_ge(s.dve_stats, n * 5 + 5)
        nc.vector.tensor_copy(w.root_wide[:], w.root[:].rearrange("p (t n) -> p t n", n=1).broadcast_to([P, KT, P]))\
            .then_inc(s.spread_ready, 1)
        dve.wait_ge(s.scale_spread, n + 1)
        for k in range(2):
            last = nc.vector.tensor_tensor(result[:, QB * k:QB * k + QB], w.centred[:, QB * k:QB * k + QB], banks[k][:],
                                           ALU.mult)
        last.then_inc(s.normal, 1)

    def project_pe(pe, b):
        hold(pe, s.normal, b * 2 + 1)
        for weight, first in ((w.wq, 0), (w.wk, 4)):
            for g in range(GROUPS):
                for k in range(2):
                    last = nc.tensor.matmul(banks[first + 2 * g + k][:], weight[:, g, :], w.z[:, QB * k:QB * k + QB],
                                            start=True, stop=True)
            last.then_inc(s.projected, 1)
        hold(pe, s.q_out, b + 1)
        for t in range(KT):
            last = nc.tensor.matmul(banks[t // 4][:, P * (t % 4):P * (t % 4) + P], w.z[:, P * t:P * t + P], w.wv[:],
                                    start=True, stop=True)
        last.then_inc(s.projected, 1)
        hold(pe, s.v_out, b + 1)

    def project_act(act, b):
        act.wait_ge(s.projected, b * 3 + 1)
        for n in range(4):
            last = nc.scalar.activation(w.q[:, n // 2, QB * (n % 2):QB * (n % 2) + QB], banks[n][:], ACT.Copy,
                                        scale=float(DH) ** -0.5)
        last.then_inc(s.q_out, 1)
        act.wait_ge(s.projected, b * 3 + 3)
        for n in range(2):
            last = nc.scalar.activation(w.v[:, 4 * n:4 * n + 4, :, 0:DH],
                                        banks[n][:].rearrange("p (t h d) -> p t h d", t=4, d=DH), ACT.Copy)
        last.then_inc(s.v_out, 1)

    def project_dve(dve, b):
        dve.wait_ge(s.projected, b * 3 + 2)
        for n in range(4):
            last = nc.vector.tensor_scalar(w.k[:, n // 2, QB * (n % 2):QB * (n % 2) + QB], banks[4 + n][:], w.row16[:],
                                           None, ALU.add)
        last.then_inc(s.k_out, 1)

    def slot(j):
        return slice(SLOT * j, SLOT * j + SLOT)

    def where(u):
        return u // 2, u % 2

    def score_pe(pe, b, u, i, reads):
        g, qb = where(u)
        t, j = i // 4, i % 4
        q0 = QB * qb + P * t
        for k in range(2):
            last = nc.tensor.matmul(banks[2 * (i % 2) + k][:], w.q[slot(j), g, q0:q0 + P],
                                    w.k[slot(j), g, QB * k:QB * k + QB], start=True, stop=True)
        last.then_inc(s.scored, 1)

    def fast_pe(pe, b):
        hold(pe, s.k_out, b + 1)
        base = b * UNITS
        for u in range(UNITS + 1):
            for i in range(16):
                if u < UNITS:
                    n = 16 * u + i
                    if i >= 2:
                        hold(pe, s.read_max, b * 64 + n - 1)
                    elif i == 0 and u >= 1:
                        hold(pe, s.shifted, base + u)
                    elif i == 1 and u >= 2:
                        hold(pe, s.den_inverse, base + u - 1)
                    score_pe(pe, b, u, i, None)
                if u >= 1:
                    g, qb = where(u - 1)
                    if u == UNITS and i == 0:
                        hold(pe, s.shifted, base + u)
                    for x in range(2 * i, 2 * i + 2):
                        kt, j = x // 4, x % 4
                        m = 32 * (u - 1) + x
                        if m >= 3:
                            hold(pe, s.exp_done, b * 128 + m - 2)
                        nc.tensor.matmul(banks[4 + m % 3][:], w.k[slot(j), g, P * kt:P * kt + P],
                                         w.q_shifted[slot(j), g, QB * qb:QB * qb + QB], start=True, stop=True)\
                            .then_inc(s.scores_t, 1)
                        if x >= 2:
                            weigh_pe(pe, b, u - 1, x - 2)
            if u >= 1:
                weigh_pe(pe, b, u - 1, 30)
                weigh_pe(pe, b, u - 1, 31)
            if u < UNITS:
                hold(pe, s.max_spread, base + u + 1)
                for t in range(4):
                    last = nc.tensor.matmul(banks[0][:, P * t:P * t + P], w.spread[:, t, :], mem.ident[:],
                                            start=True, stop=True)
                last.then_inc(s.max_turned, 1)
            if u >= 1:
                finish_pe(pe, base + u - 1)

    def weigh_pe(pe, b, u, x):
        g, _ = where(u)
        kt, j = x // 4, x % 4
        m = 32 * u + x
        hold(pe, s.exp_done, b * 128 + m + 1)
        if x == 0:
            if u >= 1:
                hold(pe, s.gathered, b * UNITS + u)
        nc.tensor.matmul(banks[7][slot(j), :], w.v[:, kt, 4 * g + j, :], w.exp[m % 4][:], start=(kt == 0),
                         stop=(kt == KT - 1)).then_inc(s.weighed, 1)

    def finish_pe(pe, n):
        hold(pe, s.gathered, n + 1)
        nc.tensor.matmul(banks[2][:], w.select[:], w.o[:], start=True, stop=True).then_inc(s.den_spread, 1)

    def finish_act(act, n, done, done_at):
        act.wait_ge(done, done_at)
        nc.scalar.activation(w.o[:], banks[7][:], ACT.Copy).then_inc(s.gathered, 1)
        act.wait_ge(s.den_spread, n + 1)
        nc.scalar.activation(w.inverse[:], banks[2][:], ACT.Ln).then_inc(s.inv_step, 1)
        act.wait_ge(s.inv_step, n + 1)
        nc.scalar.activation(w.inverse[:], w.inverse[:], ACT.Exp, scale=-1.0).then_inc(s.den_inverse, 1)

    def finish_dve(dve, b, u):
        g, qb = where(u)
        dve.wait_ge(s.den_inverse, b * UNITS + u + 1)
        nc.vector.tensor_tensor(w.att[:, g, QB * qb:QB * qb + QB], w.o[:], w.inverse[:], ALU.mult).then_inc(s.attended, 1)

    def fast_act(act, b):
        for u in range(UNITS):
            for x in range(32):
                m = 32 * u + x
                act.wait_ge(s.scores_t, b * 128 + m + 1)
                if m >= 4:
                    act.wait_ge(s.weighed, b * 128 + m - 3)
                nc.scalar.activation(w.exp[m % 4][:], banks[4 + m % 3][:], ACT.Exp).then_inc(s.exp_done, 1)
            if u >= 1:
                act.wait_ge(s.attended, b * UNITS + u)
            finish_act(act, b * UNITS + u, s.weighed, b * 128 + 32 * u + 32)

    def fast_dve(dve, b):
        for u in range(UNITS):
            g, qb = where(u)
            for i in range(16):
                hold(dve, s.scored, b * 64 + 16 * u + i + 1)
                for o in range(OCTANTS):
                    last = nc.vector.max(w.best[:, i, o, :], banks[2 * (i % 2) + o // 4][:, P * (o % 4):P * (o % 4) + P])
                last.then_inc(s.read_max, 1)
            dve.wait_ge(s.read_max, b * 64 + 16 * u + 16)
            k = Count(s.maxima, (b * UNITS + u) * 8)
            k.up(nc.vector.tensor_reduce(w.top[:], w.best[:, :, :, 0], AX.X, ALU.max))
            chained(dve, k, nc.vector.tensor_reduce(w.eighth[:], w.best[:, :, :, 7], AX.X, ALU.max))
            nc.vector.tensor_scalar(w.spread[:, :, DH:P:SLOT], w.top[:].rearrange("p (t j) -> p t j", j=4), -1.0, None,
                                    ALU.mult).then_inc(s.max_spread, 1)
            k.up(nc.vector.tensor_tensor(w.eighth[:], w.eighth[:], w.top[:], ALU.subtract))
            chained(dve, k, nc.vector.tensor_scalar(w.top[:], w.top[:], -MARGIN, None, ALU.add))
            k.up(nc.vector.scalar_tensor_tensor(w.widest[:, 0], w.eighth[:], MARGIN, w.widest[:, 0], ALU.add, ALU.max))
            near = w.best[:].rearrange("p i o e -> p i (o e)")
            chained(dve, k, nc.vector.tensor_tensor(near, near, w.top[:].rearrange("p (i n) -> p i n", n=1)
                                                    .broadcast_to([P, 16, 8 * OCTANTS]), ALU.is_gt))
            chained(dve, k, nc.vector.tensor_reduce(w.eighth[:], near, AX.X, ALU.add))
            chained(dve, k, nc.vector.scalar_tensor_tensor(w.widest[:, 1], w.eighth[:], -float(TOPK), w.widest[:, 1],
                                                           ALU.add, ALU.max))
            dve.wait_ge(s.max_turned, b * UNITS + u + 1)
            part = slice(QB * qb, QB * qb + QB)
            nc.vector.tensor_tensor(w.q_shifted[:, g, part], w.q[:, g, part], banks[0][:], ALU.add).then_inc(s.shifted, 1)
            if u >= 1:
                finish_dve(dve, b, u - 1)
        finish_dve(dve, b, UNITS - 1)

    def general_pe(pe, b):
        hold(pe, s.k_out, b + 1)
        for u in range(UNITS):
            g, _ = where(u)
            for i in range(16):
                n = 16 * u + i
                if n >= 2:
                    hold(pe, s.g_copied, (b - first) * 64 + n - 1)
                if i == 1 and u >= 1:
                    hold(pe, s.den_inverse, b * UNITS + u)
                score_pe(pe, b, u, i, None)
                hold(pe, s.g_masked, (b - first) * 64 + n + 1)
                if n >= 1:
                    hold(pe, s.g_turned_out, (b - first) * 64 + n)
                for kt in range(KT):
                    last = nc.tensor.matmul(banks[4 + kt // 4][:, P * (kt % 4):P * (kt % 4) + P],
                                            w.masked[:, P * kt:P * kt + P], mem.ident[:], start=True, stop=True)
                last.then_inc(s.g_turned, 1)
                hold(pe, s.g_turned_out, (b - first) * 64 + n + 1)
                if i == 0 and u >= 1:
                    hold(pe, s.gathered, b * UNITS + u)
                t, j = i // 4, i % 4
                for kt in range(KT):
                    last = nc.tensor.matmul(banks[7][slot(j), P * t:P * t + P], w.v[:, kt, 4 * g + j, :],
                                            w.turned[:, kt, :], start=(kt == 0), stop=(kt == KT - 1))
                last.then_inc(s.g_pv, 1)
            finish_pe(pe, b * UNITS + u)

    def general_act(act, b):
        for u in range(UNITS):
            for i in range(16):
                n = 16 * u + i
                act.wait_ge(s.scored, b * 64 + n + 1)
                for k in range(2):
                    last = nc.scalar.activation(w.scores[:, QB * k:QB * k + QB], banks[2 * (i % 2) + k][:], ACT.Copy)
                last.then_inc(s.g_copied, 1)
                act.wait_ge(s.g_ranked, (b - first) * 64 + n + 1)
                nc.scalar.activation(w.masked[:], w.scores[:], ACT.Exp, bias=w.minus_top[:]).then_inc(s.g_exp, 1)
                act.wait_ge(s.g_turned, (b - first) * 64 + n + 1)
                if n >= 1:
                    act.wait_ge(s.g_pv, (b - first) * 64 + n)
                for k in range(2):
                    last = nc.scalar.activation(w.turned[:, 4 * k:4 * k + 4, :].rearrange("p k n -> p (k n)"),
                                                banks[4 + k][:], ACT.Copy)
                last.then_inc(s.g_turned_out, 1)
            if u >= 1:
                act.wait_ge(s.attended, b * UNITS + u)
            finish_act(act, b * UNITS + u, s.g_pv, (b - first) * 64 + 16 * u + 16)

    def general_dve(dve, b):
        for u in range(UNITS):
            for i in range(16):
                n = 16 * u + i
                hold(dve, s.g_copied, (b - first) * 64 + n + 1)
                k = Count(s.rank_steps, ((b - first) * 64 + n) * 8)
                source = w.scores
                for r in range(TOPK // 8):
                    chained(dve, k, nc.vector.max(w.eight[:, r, :], source[:]))
                    chained(dve, k, nc.vector.match_replace(w.rest[:], w.eight[:, r, :], source[:], NEGATIVE))
                    source = w.rest
                nc.vector.tensor_scalar(w.minus_top[:], w.eight[:, 0, 0:1], -1.0, None, ALU.mult).then_inc(s.g_ranked, 1)
                dve.wait_ge(s.g_exp, (b - first) * 64 + n + 1)
                nc.vector.scalar_tensor_tensor(w.masked[:], w.rest[:], NEGATIVE, w.masked[:], ALU.is_equal, ALU.mult)\
                    .then_inc(s.g_masked, 1)
            finish_dve(dve, b, u)

    def join_pe(pe, b):
        hold(pe, s.attended, (b + 1) * UNITS)
        for k in range(2):
            for g in range(GROUPS):
                last = nc.tensor.matmul(banks[4 + k][:], w.wo[:, g, :], w.att[:, g, QB * k:QB * k + QB],
                                        start=(g == 0), stop=(g == GROUPS - 1))
        last.then_inc(s.joined, 1)

    def join_dve(dve, b):
        dve.wait_ge(s.joined, b + 1)
        with_b(dve, b)
        for k in range(2):
            part = slice(QB * k, QB * k + QB)
            last = nc.vector.scalar_tensor_tensor(w.t[:, part], banks[4 + k][:], w.bo[:], tokens(b)[:, part],
                                                  ALU.add, ALU.add)
        last.then_inc(s.residual, 1)

    def with_b(dve, b):
        hold(dve, s.stored, (b + 1) * 16)

    def experts_pe(pe, b):
        hold(pe, s.normal, b * 2 + 2)
        for t in range(KT):
            last = nc.tensor.matmul(banks[2][:, 8 * t:8 * t + EXPERTS + 1], w.z[:, P * t:P * t + P], w.gates_t[:],
                                    start=True, stop=True)
        last.then_inc(s.gated, 1)
        n = 0
        for k in range(2):
            for e in range(EXPERTS):
                if n >= 2:
                    out = s.hidden_act if n % 2 == 0 else s.hidden_dve
                    hold(pe, out, b * 4 + n // 2)
                nc.tensor.matmul(banks[n % 2][:], w.fc1t[:, e, :], w.z[:, QB * k:QB * k + QB], start=True, stop=True)\
                    .then_inc(s.hidden, 1)
                n += 1
        for k in range(2):
            for e in range(EXPERTS):
                n = EXPERTS * k + e
                hold(pe, s.hidden_act if n % 2 == 0 else s.hidden_dve, b * 4 + n // 2 + 1)
                last = nc.tensor.matmul(banks[4 + k][0:LORA, :], w.lora_a[:, e, :], w.hid[:, n, :],
                                        start=(e == 0), stop=(e == EXPERTS - 1))
            last.then_inc(s.low, 1)
        hold(pe, s.gate_done, b + 1)
        for t in range(KT):
            last = nc.tensor.matmul(banks[6 + t // 4][0:LORA, P * (t % 4):P * (t % 4) + P], w.gate_wide[:, t, :],
                                    mem.ident[:], start=True, stop=True)
        last.then_inc(s.gates_t_done, 1)
        hold(pe, s.mixed_low, b + 1)
        for k in range(2):
            last = nc.tensor.matmul(banks[k][:], w.lora_out[:], w.low[:, k, :], start=True, stop=True)
        last.then_inc(s.expert_out, 1)

    def experts_act(act, b):
        act.wait_ge(s.gated, b + 1)
        act.wait_ge(s.gate_steps, b * GATE_STEPS + 3)
        nc.scalar.activation(w.gate[:, :, 0:EXPERTS], w.gate[:, :, 0:EXPERTS], ACT.Exp)
        nc.scalar.activation(w.threshold[:], w.threshold[:], ACT.Exp, scale=-1.0).then_inc(s.gate_exp, 1)
        for n in range(0, 2 * EXPERTS, 2):
            act.wait_ge(s.hidden, b * 8 + n + 1)
            nc.scalar.activation(w.hid[:, n, :], banks[0][:], ACT.Relu).then_inc(s.hidden_act, 1)
        for k in range(2):
            act.wait_ge(s.low, b * 2 + k + 1)
            last = nc.scalar.activation(w.low[:, k, :], banks[4 + k][0:LORA, :], ACT.Copy)
        last.then_inc(s.low_out, 1)

    GATE_STEPS = 13

    def experts_dve(dve, b):
        k = Count(s.gate_steps, b * GATE_STEPS)
        gate = w.gate[:, :, 0:EXPERTS]
        logits = banks[2][:, 0:8 * KT].rearrange("p (t x) -> p t x", x=8)[:, :, 0:EXPERTS]

        def over(t):
            return t.rearrange("p (t n) -> p t n", n=1).broadcast_to([P, KT, EXPERTS])

        dve.wait_ge(s.gated, b + 1)
        k.up(nc.vector.tensor_scalar(w.threshold[:], banks[2][:, 0:8 * KT].rearrange("p (t x) -> p t x", x=8)[:, :, EXPERTS],
                                     -87.0, None, ALU.max))
        chained(dve, k, nc.vector.tensor_reduce(w.gate_sum[:], logits, AX.X, ALU.max))
        chained(dve, k, nc.vector.tensor_tensor(gate, logits, over(w.gate_sum[:]), ALU.subtract))
        for n in range(1, 2 * EXPERTS, 2):
            dve.wait_ge(s.hidden, b * 8 + n + 1)
            nc.vector.tensor_scalar(w.hid[:, n, :], banks[1][:], 0.0, None, ALU.max).then_inc(s.hidden_dve, 1)
        dve.wait_ge(s.gate_exp, b + 1)
        k.up(nc.vector.tensor_scalar(w.threshold[:], w.threshold[:], 1.0, float(EXPERTS), ALU.add, ALU.mult))
        chained(dve, k, nc.vector.tensor_reduce(w.gate_sum[:], gate, AX.X, ALU.add))
        k.up(nc.vector.reciprocal(w.threshold[:], w.threshold[:]))
        chained(dve, k, nc.vector.reciprocal(w.gate_sum[:], w.gate_sum[:]))
        chained(dve, k, nc.vector.tensor_tensor(gate, gate, over(w.gate_sum[:]), ALU.mult))
        chained(dve, k, nc.vector.tensor_tensor(gate, gate, over(w.threshold[:]), ALU.subtract))
        chained(dve, k, nc.vector.tensor_scalar(gate, gate, 0.0, None, ALU.max))
        chained(dve, k, nc.vector.tensor_reduce(w.gate_sum[:], gate, AX.X, ALU.add))
        chained(dve, k, nc.vector.scalar_tensor_tensor(w.gate_sum[:], w.gate_sum[:], 0.0, w.gate_sum[:], ALU.is_equal,
                                                       ALU.add))
        chained(dve, k, nc.vector.reciprocal(w.gate_sum[:], w.gate_sum[:]))
        nc.vector.tensor_tensor(gate, gate, over(w.gate_sum[:]), ALU.mult).then_inc(s.mixed, 1)
        dve.wait_ge(s.mixed, b + 1)
        nc.vector.tensor_copy(w.gate_wide[:].rearrange("p t (e r) -> p t e r", r=RANK),
                              w.gate[:, :, 0:EXPERTS].rearrange("p t (e n) -> p t e n", n=1)
                              .broadcast_to([P, KT, EXPERTS, RANK])).then_inc(s.gate_done, 1)
        dve.wait_ge(s.low_out, b + 1)
        dve.wait_ge(s.gates_t_done, b + 1)
        for n in range(2):
            last = nc.vector.tensor_tensor(w.low[:, n, :], w.low[:, n, :], banks[6 + n][0:LORA, :], ALU.mult)
        last.then_inc(s.mixed_low, 1)
        dve.wait_ge(s.expert_out, b + 1)
        for n in range(2):
            part = slice(QB * n, QB * n + QB)
            last = nc.vector.tensor_tensor(w.t[:, part], w.t[:, part], banks[n][:], ALU.add)
        last.then_inc(s.finished, 1)

    def pe_image(pe, b):
        norm_pe(pe, b * 2, tokens(b))
        project_pe(pe, b)
        (general_pe if general else fast_pe)(pe, b)
        join_pe(pe, b)
        hold(pe, s.residual, b + 1)
        norm_pe(pe, b * 2 + 1, w.t)
        experts_pe(pe, b)
        hold(pe, s.finished, b + 1)

    def act_image(act, b):
        norm_act(act, b * 2)
        project_act(act, b)
        (general_act if general else fast_act)(act, b)
        norm_act(act, b * 2 + 1)
        experts_act(act, b)

    def dve_image(dve, b):
        norm_dve(dve, b * 2, tokens(b), w.z)
        project_dve(dve, b)
        (general_dve if general else fast_dve)(dve, b)
        join_dve(dve, b)
        norm_dve(dve, b * 2 + 1, w.t, w.z)
        experts_dve(dve, b)

    def sp_image(sp, b):
        sp.wait_ge(s.finished, b + 1)
        sp.dma_start(out_dram[:, bass.ds(b - first, 1), :], w.t[:].rearrange("p (m n) -> p m n", m=1)).then_inc(s.stored, 16)

    return pe_image, act_image, dve_image, sp_image


def attention_and_experts(nc, mem, w, out_dram):
    with ExitStack() as ctx:
        s = PassSemaphores(lambda name: ctx.enter_context(nc.semaphore(name)))
        usual, general = (image_pass(nc, mem, w, s, out_dram, which) for which in (False, True))
        widest_ready, widest_turned, flag_ready = (ctx.enter_context(nc.semaphore(n)) for n in
                                                   ("widest_ready", "widest_turned", "flag_ready"))
        block = ctx.enter_context(nc.Block())

        def once(eng, n):
            with eng.Fori(0, B) as b:
                usual[n](eng, b)

        def again(eng, n):
            eng.wait_ge(flag_ready, 1)
            flag = eng.value_load(mem.flag[0:1, 0:1], min_val=0, max_val=1)
            with eng.If(flag > 0):
                with eng.Fori(B, 2 * B) as b:
                    general[n](eng, b)
                if n == 3:
                    eng.wait_ge(s.stored, 16 * (2 * B + 1))

        @block.tensor
        def _(pe):
            once(pe, 0)
            pe.wait_ge(widest_ready, 1)
            nc.tensor.matmul(mem.banks[0][0:1, 0:P], w.top[:, 0:1], mem.ident[:], start=True, stop=True)\
                .then_inc(widest_turned, 1)
            again(pe, 0)

        @block.scalar
        def _(act):
            nc.scalar.preload_act_table_set("natural_log_exp_and_others")
            once(act, 1)
            again(act, 1)

        @block.vector
        def _(dve):
            once(dve, 2)
            nc.vector.tensor_reduce(w.top[:, 0:1], w.widest[:].rearrange("p a b -> p (a b)"), AX.X, ALU.max)\
                .then_inc(widest_ready, 1)
            dve.wait_ge(widest_turned, 1)
            nc.vector.tensor_reduce(w.eighth[0:1, 0:1], mem.banks[0][0:1, 0:P], AX.X, ALU.max).then_inc(widest_ready, 1)
            dve.wait_ge(widest_ready, 2)
            nc.vector.tensor_scalar(mem.flag[0:1, 0:1], w.eighth[0:1, 0:1], 0.0, None, ALU.is_gt).then_inc(flag_ready, 1)
            again(dve, 2)

        @block.sync
        def _(sp):
            sp.sem_inc(s.stored, 16)
            once(sp, 3)
            sp.wait_ge(s.stored, 16 * (B + 1))
            again(sp, 3)





def hybrid_kernel(nc, dram, out):
    x_dram = dram["x"].rearrange("b c h w -> c b (h w)")
    out_dram = out.rearrange("b c h w -> c b (h w)")
    with ExitStack() as ctx:
        mem = Memory()

        def sb(name, shape):
            return ctx.enter_context(nc.sbuf_tensor(name, shape, F32))

        mem.flag = ctx.enter_context(nc.sbuf_tensor("flag", [1, 1], mybir.dt.int32))
        mem.ident = sb("ident", [P, P])
        mem.group = sb("group", [P, P])
        mem.quad_mean = sb("quad_mean", [P, P])
        mem.tiny = sb("tiny", [P, 1])
        mem.eps_gn = sb("eps_gn", [P, 1])
        mem.minus_tiny, mem.tiny_log = sb("minus_tiny", [P, 1]), sb("tiny_log", [P, 1])
        mem.one, mem.two, mem.half = (sb(n, [P, HB, PAIRS]) for n in ("one", "two", "half"))
        mem.shift = sb("shift", [P, B])
        mem.even = sb("even", [P, B, N])
        mem.banks = [ctx.enter_context(nc.psum_tensor(f"bank{i}", [P, 512], F32)) for i in range(8)]
        mem.dots = mem.banks[0:2]
        Passed.sem = ctx.enter_context(nc.semaphore("passed"))
        constants(nc, mem)
        with ExitStack() as first:
            mem.odd = first.enter_context(nc.sbuf_tensor("odd", [P, B, N], F32))
            with ExitStack() as spectral:
                mem.weights = spectral.enter_context(nc.sbuf_tensor("weights", [P, 2, 2, HB, S], F32))
                mem.work = spectral.enter_context(nc.sbuf_tensor("work", [P, 3, HB * PAIRS * S], F32))
                mem.product = [mem.work[:, 0], mem.work[:, 2]]
                normalise(nc, mem, x_dram)
                jacobi(nc, mem)
                logarithm(nc, mem)
            exponential(nc, mem, dram["gamma"], dram["beta"])
            mem.work = first.enter_context(nc.sbuf_tensor("work2", [P, 2, HB * PAIRS * S], F32))
            back_to_channels(nc, mem, x_dram)
        w = Tiles(sb)
        load_weights(nc, mem, w, dram)
        attention_and_experts(nc, mem, w, out_dram)


INPUTS = dict(x="x", gamma="L0_conv_gamma", beta="L0_conv_beta", wq="L1_attn_Wq", wk="L1_attn_Wk", wv="L1_attn_Wv",
              wo="L1_attn_Wo", bo="L1_attn_bo", gate="L1_ffn_gate_w", thr="L1_ffn_thr_w", fc1="L1_ffn_fc1_w",
              lora_a="L1_ffn_lora_A", lora_b="L1_ffn_lora_B", fc2="L1_ffn_fc2_w")


def kernel(**inputs):
    import numpy as np
    import concourse.bacc as bacc
    from concourse.bass_utils import run_bass_kernel_spmd as run

    nc = bacc.Bacc("TRN2", target_bir_lowering=False, num_devices=1)
    arrays, dram = {}, {}
    for name, source in INPUTS.items():
        arrays[f"in_{name}"] = np.ascontiguousarray(inputs[source])
        dram[name] = nc.dram_tensor(f"in_{name}", arrays[f"in_{name}"].shape, F32, kind="ExternalInput").ap()
    out = nc.dram_tensor("out_0", (B, P, S, S), F32, kind="ExternalOutput").ap()
    hybrid_kernel(nc, dram, out)
    r = run(nc, [arrays], core_ids=[0])
    return r.results[0]["out_0"]
```

```python
import math
from contextlib import ExitStack

import concourse.bass as bass
from concourse import mybir

F32 = mybir.dt.float32
BF16 = mybir.dt.bfloat16
ALU = mybir.AluOpType
ACT = mybir.ActivationFunctionType
AX = mybir.AxisListType

P = 128
B = 16
S = 32
N = S * S
HB = B // 2
BY_PE = 2
PAIRS = S // 2
ROUNDS = S - 1
SWEEPS = 6
EPS_LOG = 1e-8
GROUP = 4
EPS_GN = 1e-5
TINY = 1e-30
TINY_LOG = 1e-18
SQUARINGS = 7
TAYLOR = [1.0 / math.factorial(n) for n in range(7)]
QUADS = B // 4


class Memory:
    pass


class Count:

    def __init__(self, sem, base=0):
        self.sem, self.base, self.n = sem, base, 0

    def up(self, ins, by=1):
        self.n += by
        ins.then_inc(self.sem, by)
        return self.value()

    def value(self):
        return self.base + self.n


def chained(eng, count, ins):
    hold(eng, count.sem, count.up(ins))


def hold(eng, sem, value):
    eng.wait_ge(sem, value)
    eng.sem_inc(Passed.sem, 1)


class Passed:
    sem = None


def refine_root(nc, eng, sem, at, root, of, spare):
    nc.vector.reciprocal(spare, root).then_inc(sem, 1)
    eng.wait_ge(sem, at + 1)
    nc.vector.tensor_tensor(spare, spare, of, ALU.mult).then_inc(sem, 1)
    eng.wait_ge(sem, at + 2)
    nc.vector.tensor_tensor(root, root, spare, ALU.add).then_inc(sem, 1)
    eng.wait_ge(sem, at + 3)
    nc.vector.tensor_scalar(root, root, 0.5, None, ALU.mult).then_inc(sem, 1)
    eng.wait_ge(sem, at + 4)


def constants(nc, mem):
    with ExitStack() as ctx:
        filled = ctx.enter_context(nc.semaphore("filled"))
        block = ctx.enter_context(nc.Block())

        @block.gpsimd
        def _(pool):
            nc.gpsimd.memset(mem.ident[:], 0.0).then_inc(filled, 1)
            nc.gpsimd.memset(mem.group[:], 1.0 / (GROUP * N)).then_inc(filled, 1)
            nc.gpsimd.memset(mem.quad_mean[:], 0.0).then_inc(filled, 1)
            nc.gpsimd.memset(mem.tiny[:], TINY).then_inc(filled, 1)
            nc.gpsimd.memset(mem.eps_gn[:], EPS_GN).then_inc(filled, 1)
            for tile, value in ((mem.minus_tiny, -TINY), (mem.tiny_log, TINY_LOG), (mem.one, 1.0), (mem.two, 2.0)):
                nc.gpsimd.memset(tile[:], value)
            hold(pool, filled, 5)
            nc.gpsimd.affine_select(out=mem.ident[:], in_=mem.ident[:], compare_op=ALU.not_equal, fill=1.0,
                                    base=0, pattern=[[-1, P]], channel_multiplier=1).then_inc(filled, 1)
            gv = mem.group[:].rearrange("p (g c) -> p g c", c=GROUP)
            nc.gpsimd.affine_select(out=gv, in_=gv, compare_op=ALU.is_ge, fill=0.0, base=0,
                                    pattern=[[-GROUP, P // GROUP], [0, GROUP]], channel_multiplier=1).then_inc(filled, 1)
            hold(pool, filled, 7)
            nc.gpsimd.affine_select(out=gv, in_=gv, compare_op=ALU.is_ge, fill=0.0, base=GROUP - 1,
                                    pattern=[[GROUP, P // GROUP], [0, GROUP]], channel_multiplier=-1).then_inc(filled, 1)
            for d in range(-3, 4):
                hold(pool, filled, 8 + d + 3)
                nc.gpsimd.affine_select(out=mem.quad_mean[:], in_=mem.quad_mean[:], compare_op=ALU.not_equal,
                                        fill=1.0 / (B * P), base=S * d, pattern=[[-1, P]],
                                        channel_multiplier=1).then_inc(filled, 1)


def column_norms(nc, mem, sems, base):
    squares_ready, norms_summed = sems

    def act_part(act, source_ready, ready_at, norms_ready):
        for c in range(4):
            act.wait_ge(source_ready, ready_at[c // 2])
            if c >= 2:
                act.wait_ge(norms_summed, base * 4 + c - 1)
            nc.scalar.activation(mem.product[c % 2][:, :].rearrange("p (m n) -> p m n", m=4),
                                 mem.even[:, 4 * c:4 * c + 4, :], ACT.Square).then_inc(squares_ready, 1)
            if c >= 1:
                collect(act, c - 1, norms_ready)
        collect(act, 3, norms_ready)

    def collect(act, c, norms_ready):
        act.wait_ge(norms_summed, base * 4 + c + 1)
        nc.scalar.activation(mem.weights[:, c // 2, 0, 4 * (c % 2):4 * (c % 2) + 4, :],
                             mem.dots[c % 2][:, 0:4 * S].rearrange("p (m j) -> p m j", m=4),
                             ACT.Copy).then_inc(norms_ready, 1)

    def pe_part(pe, norms_ready, ready_base):
        for c in range(4):
            hold(pe, squares_ready, base * 4 + c + 1)
            if c >= 2:
                hold(pe, norms_ready, ready_base + c - 1)
            sq = mem.product[c % 2][:, :].rearrange("p (mj r) -> p mj r", r=S)
            for r in range(S):
                last = nc.tensor.matmul(mem.dots[c % 2][:, 0:4 * S], mem.ident[:], sq[:, :, r],
                                        start=(r == 0), stop=(r == S - 1))
            last.then_inc(norms_summed, 1)

    return act_part, pe_part


def normalise(nc, mem, x_dram):
    with ExitStack() as ctx:
        def sem(name):
            return ctx.enter_context(nc.semaphore(name))

        loaded, step, act_done, pe_done = sem("x_loaded"), sem("prep_step"), sem("prep_act"), sem("prep_pe")
        squared, refined = sem("prep_squared"), sem("prep_refined")
        norm_sems = (sem("prep_squares"), sem("prep_norms"))
        norms_ready = sem("prep_norms_ready")
        sums = ctx.enter_context(nc.sbuf_tensor("sums", [P, 4, B], F32))
        ps = mem.dots[0]
        block = ctx.enter_context(nc.Block())
        tr = "p m (c r) -> p m r c"

        @block.sync
        def _(sp):
            sp.dma_start(mem.odd[:], x_dram).then_inc(loaded, 16)

        @block.tensor
        def _(pe):
            hold(pe, step, 1)
            nc.tensor.matmul(ps[:, 0:B], mem.group[:], sums[:, 0, :], start=True, stop=True).then_inc(pe_done, 1)
            pe.wait_ge(squared, B)
            nc.tensor.matmul(ps[:, B:2 * B], mem.group[:], sums[:, 1, :], start=True, stop=True).then_inc(pe_done, 1)
            column_norms(nc, mem, norm_sems, 0)[1](pe, norms_ready, 0)
            column_norms(nc, mem, norm_sems, 1)[1](pe, norms_ready, 4)

        @block.scalar
        def _(act):
            act.wait_ge(step, 2)
            scratch = mem.work[:].rearrange("p s (m n) -> p (s m) n", n=N)
            for m in range(B):
                if m >= 12:
                    act.wait_ge(squared, m - 11)
                nc.scalar.activation(scratch[:, m % 12, :], mem.even[:, m, :], ACT.Square,
                                     accum_out=sums[:, 1, m:m + 1]).then_inc(squared, 1)
            act.wait_ge(pe_done, 2)
            nc.scalar.activation(sums[:, 2, :], ps[:, B:2 * B], ACT.Sqrt, bias=mem.eps_gn[:]).then_inc(act_done, 1)
            column_norms(nc, mem, norm_sems, 0)[0](act, step, (6, 6), norms_ready)
            act.wait_ge(step, 7)
            nc.scalar.activation(sums[:, 3, :], sums[:, 2, :], ACT.Sqrt, bias=mem.tiny[:]).then_inc(act_done, 1)
            column_norms(nc, mem, norm_sems, 1)[0](act, step, (9, 9), norms_ready)

        @block.vector
        def _(dve):
            dve.wait_ge(loaded, 16)
            nc.vector.tensor_reduce(sums[:, 0, :], mem.odd[:], AX.X, ALU.add).then_inc(step, 1)
            dve.wait_ge(pe_done, 1)
            nc.vector.tensor_tensor(mem.even[:], mem.odd[:],
                                    ps[:, 0:B].rearrange("p (m n) -> p m n", n=1).broadcast_to([P, B, N]),
                                    ALU.subtract).then_inc(step, 1)
            dve.wait_ge(step, 2)
            nc.vector.tensor_tensor(mem.odd[:].rearrange("p m (r c) -> p m r c", r=S),
                                    mem.even[:].rearrange("p m (r c) -> p m r c", r=S),
                                    mem.even[:].rearrange(tr, c=S), ALU.add).then_inc(step, 1)
            dve.wait_ge(act_done, 1)
            nc.vector.tensor_scalar(sums[:, 0, :], ps[:, B:2 * B], EPS_GN, None, ALU.add).then_inc(refined, 1)
            dve.wait_ge(refined, 1)
            refine_root(nc, dve, refined, 1, sums[:, 2, :], sums[:, 0, :], sums[:, 1, :])
            nc.vector.reciprocal(sums[:, 0, :], sums[:, 2, :]).then_inc(step, 1)
            dve.wait_ge(step, 4)
            nc.vector.tensor_scalar(sums[:, 1, :], sums[:, 0, :], 0.5, None, ALU.mult).then_inc(step, 1)
            dve.wait_ge(step, 5)
            nc.vector.tensor_tensor(mem.even[:], mem.odd[:],
                                    sums[:, 1, :].rearrange("p (m n) -> p m n", n=1).broadcast_to([P, B, N]),
                                    ALU.mult).then_inc(step, 1)
            dve.wait_ge(norms_ready, 4)
            for h in range(2):
                last = nc.vector.tensor_reduce(sums[:, 2, HB * h:HB * h + HB], mem.weights[:, h, 0], AX.X, ALU.add)
            last.then_inc(step, 1)
            dve.wait_ge(act_done, 2)
            nc.vector.tensor_scalar(mem.shift[:], sums[:, 3, :], 1.1, 1e-4, ALU.mult, ALU.add).then_inc(step, 1)
            dve.wait_ge(step, 8)
            diag = mem.even[:, :, 0:N:S + 1]
            nc.vector.tensor_tensor(diag, diag, mem.shift[:].rearrange("p (m n) -> p m n", n=1).broadcast_to([P, B, S]),
                                    ALU.add).then_inc(step, 1)


def jacobi(nc, mem):
    with ExitStack() as ctx:
        def sem(name):
            return ctx.enter_context(nc.semaphore(name))

        def small(name, *shape):
            return ctx.enter_context(nc.sbuf_tensor(name, [P, 2] + list(shape), F32))

        twice_dot = small("twice_dot", HB, PAIRS)
        weighed = small("weighed", HB, 2, PAIRS)
        cross = small("cross", HB, PAIRS)
        half_cross = small("half_cross", HB, PAIRS)
        gap = small("gap", HB, PAIRS)
        radicand = small("radicand", HB, PAIRS)
        root = small("root", HB, PAIRS)
        gap_abs = small("gap_abs", HB, PAIRS)
        gap_sign = small("gap_sign", 2, HB, PAIRS)
        inverse = small("inverse", HB, PAIRS)
        ratio = small("ratio", 2, HB, PAIRS)
        coef = small("coef", HB, 2, PAIRS)
        secant = small("secant", HB, PAIRS)
        cosine = small("cosine", HB, PAIRS)
        moved = small("moved", 2, HB, S)
        scale = small("scale", HB, S)

        prod_ready = [sem(f"prod_ready{h}") for h in range(2)]
        dots_done = [sem(f"dots_done{h}") for h in range(2)]
        dot_read = [sem(f"dot_read{h}") for h in range(2)]
        cross_ready = [sem(f"cross_ready{h}") for h in range(2)]
        gap_ready = [sem(f"gap_ready{h}") for h in range(2)]
        root_ready = [sem(f"root_ready{h}") for h in range(2)]
        sum_ready = [sem(f"sum_ready{h}") for h in range(2)]
        inverse_ready = [sem(f"inverse_ready{h}") for h in range(2)]
        act_step = sem("act_step")
        coef_ready = [sem(f"coef_ready{h}") for h in range(2)]
        sec_ready = [sem(f"sec_ready{h}") for h in range(2)]
        cos_ready = [sem(f"cos_ready{h}") for h in range(2)]
        moved_ready = [sem(f"moved_ready{h}") for h in range(2)]
        weights_ready = [sem(f"weights_ready{h}") for h in range(2)]
        part_ready = [sem(f"part_ready{h}") for h in range(2)]
        rotated_ready = [sem(f"rotated_ready{h}") for h in range(2)]
        rotated_out = [sem(f"rotated_out{h}") for h in range(2)]
        ones_ready = sem("ones_ready")
        left_over = sem("left_over")
        scale_log = sem("scale_log")
        scale_ready = sem("scale_ready")
        scaled = sem("scaled")
        norms_ready = sem("norms_ready")
        norm_sems = (sem("squares_ready"), sem("norms_summed"))
        dve_step, pool_step = sem("dve_step"), sem("pool_step")
        DVE_STEPS, POOL_STEPS, ACT_STEPS = 8, 18, 6

        def columns(buf, h):
            return buf[:, HB * h:HB * h + HB, :].rearrange("p m (j r) -> p m j r", r=S)

        def paired(buf, h):
            return buf[:, HB * h:HB * h + HB, :].rearrange("p m (s j r) -> p m s j r", s=2, r=S)

        def swapped(t):
            return t[:, :, ::-1]

        def over_sides(t):
            return t.rearrange("p m (s j) -> p m s j", s=1).broadcast_to([P, HB, 2, PAIRS])

        def twice(t):
            return t.rearrange("p m (s j) -> p s m j", s=1).broadcast_to([P, 2, HB, PAIRS])

        def places(src, dst):
            inner = dst[:, :, 2:S - 2]
            return [(inner, src[:, :, :, 1:PAIRS - 1]), (dst[:, :, 0:2], src[:, :, :, 0]),
                    (dst[:, :, S - 1:S - 3:-1], src[:, :, :, PAIRS - 1])]

        block = ctx.enter_context(nc.Block())

        mine, others = slice(0, HB - BY_PE), slice(HB - BY_PE, HB)
        rotated = mem.psum[:, 2:2 + 2 * BY_PE, :].rearrange("p (m s) (j r) -> p m s j r", s=2, r=S)

        def partners(h):
            part = (mem.work[:, 0:2] if h == 0 else mem.work[:, 2:0:-1])
            return part.rearrange("p s (m j r) -> p m s j r", m=HB, r=S)

        @block.vector
        def _(dve):
            def products(h, buf, put_at=None):
                g = paired(buf, h)
                product = mem.product[h][:, :].rearrange("p (m j r) -> p m j r", m=HB, r=S)
                for which in (mine, others):
                    if which is others and put_at is not None:
                        dve.wait_ge(rotated_out[h], put_at)
                    nc.vector.tensor_tensor(product[:, which], g[:, which, 0], g[:, which, 1], ALU.mult)\
                        .then_inc(prod_ready[h], 1)

            def round_(k, src, dst, last=False):
                step = Count(dve_step, k * DVE_STEPS)
                for h in range(2):
                    part = partners(h)
                    dve.wait_ge(coef_ready[h], k + 1)
                    cb = coef[:, h].rearrange("p m s (j r) -> p m s j r", r=1).broadcast_to([P, HB, 2, PAIRS, S])
                    partner = swapped(paired(src, h))
                    for which in ((mine, others) if last else (others, mine)):
                        if which is others and last and h == 1:
                            dve.wait_ge(rotated_out[0], k + 1)
                        ins = nc.vector.tensor_tensor(part[:, which], partner[:, which], cb[:, which], ALU.mult)
                        if which is others:
                            ins.then_inc(part_ready[h], 1)
                        else:
                            chained(dve, step, ins)
                    part = part[:, mine]
                    g, d = paired(src, h)[:, mine], columns(dst, h)[:, mine]
                    for n, ((to, a), (_, b)) in enumerate(zip(places(g, d), places(part, d))):
                        if n == 0:
                            to = to.rearrange("p m (s j) r -> p m s j r", s=2)
                        ins = nc.vector.tensor_tensor(to, a, b, ALU.add)
                        if n < 2:
                            step.up(ins)
                        else:
                            chained(dve, step, ins)
                    if not last:
                        products(h, dst, k + 1)

            with dve.Fori(0, SWEEPS) as sw:
                k0 = sw * ROUNDS
                for h in range(2):
                    products(h, mem.even)
                with dve.Fori(0, ROUNDS // 2) as i:
                    round_(k0 + i * 2, mem.even, mem.odd)
                    round_(k0 + i * 2 + 1, mem.odd, mem.even)
                round_(k0 + ROUNDS - 1, mem.even, mem.odd, last=True)
                w = mem.weights
                for h in range(2):
                    dve.wait_ge(rotated_out[h], (sw + 1) * ROUNDS)
                    dve.wait_ge(scale_ready, sw * 2 + h + 1)
                    for n, ins in enumerate((lambda: nc.vector.tensor_tensor(moved[:, h, 0], scale[:, h], scale[:, h], ALU.mult),
                                             lambda: nc.vector.reciprocal(moved[:, h, 0], moved[:, h, 0]),
                                             lambda: nc.vector.tensor_tensor(w[:, h, 1], w[:, h, 1], moved[:, h, 0], ALU.mult))):
                        ins().then_inc(left_over, 1)
                        dve.wait_ge(left_over, sw * 6 + h * 3 + n + 1)
                    sb = scale[:, h].rearrange("p m (j r) -> p m j r", r=1).broadcast_to([P, HB, S, S])
                    nc.vector.tensor_tensor(columns(mem.even, h), columns(mem.odd, h), sb, ALU.mult).then_inc(scaled, 1)
                dve.wait_ge(scaled, sw * 2 + 2)
                dve.wait_ge(norms_ready, sw * 4 + 4)

        @block.tensor
        def _(pe):
            def dots(k, h):
                hold(pe, prod_ready[h], (k + 1) * 2)
                pr = mem.product[h][:, :].rearrange("p (mj r) -> p mj r", r=S)
                for r in range(S):
                    last = nc.tensor.matmul(mem.dots[h][:, 0:P], mem.ident[:], pr[:, :, r],
                                            start=(r == 0), stop=(r == S - 1))
                last.then_inc(dots_done[h], 1)

            def rotate(k, h, src):
                hold(pe, part_ready[h], k + 1)
                for m in range(HB - BY_PE, HB):
                    for side in range(2):
                        to = mem.banks[2 + 2 * (m - HB + BY_PE) + side]
                        for n, of in enumerate((paired(src, h), partners(h))):
                            last = nc.tensor.matmul(to, mem.ident[:], of[:, m, side].rearrange("p j r -> p (j r)"),
                                                    start=(n == 0), stop=(n == 1))
                last.then_inc(rotated_ready[h], 1)

            def round_(k, src, before):
                dots(k, 0)
                if before is not None:
                    rotate(k - 1, 1, before)
                dots(k, 1)
                rotate(k, 0, src)

            with pe.Fori(0, SWEEPS) as sw:
                k0 = sw * ROUNDS
                round_(k0, mem.even, None)
                with pe.Fori(0, ROUNDS // 2) as i:
                    round_(k0 + i * 2 + 1, mem.odd, mem.even)
                    round_(k0 + i * 2 + 2, mem.even, mem.odd)
                rotate(k0 + ROUNDS - 1, 1, mem.even)
                column_norms(nc, mem, norm_sems, sw)[1](pe, norms_ready, sw * 4)

        @block.scalar
        def _(act):
            def put_rotated(k, h, dst):
                act.wait_ge(rotated_ready[h], k + 1)
                for n, (to, a) in enumerate(places(rotated, columns(dst, h)[:, others])):
                    if n == 0:
                        to = to.rearrange("p m (s j) r -> p m s j r", s=2)
                    last = nc.scalar.activation(to, a, ACT.Copy)
                last.then_inc(rotated_out[h], 1)

            def round_(k, src, dst, first=False):
                step = Count(act_step, k * ACT_STEPS)
                for h in range(2):
                    act.wait_ge(gap_ready[h], k + 1)
                    nc.scalar.activation(radicand[:, h], gap[:, h], ACT.Square)
                    nc.scalar.activation(gap_abs[:, h], gap[:, h], ACT.Abs)
                    nc.scalar.activation(gap_sign[:, h, 1], gap[:, h], ACT.Sign, bias=mem.tiny[:])
                    nc.scalar.activation(gap_sign[:, h, 0], gap[:, h], ACT.Sign, scale=-1.0, bias=mem.minus_tiny[:])
                    act.wait_ge(dots_done[h], k + 1)
                    nc.scalar.activation(twice_dot[:, h].rearrange("p m j -> p (m j)"), mem.dots[h][:, 0:P], ACT.Copy,
                                         scale=2.0).then_inc(dot_read[h], 1)
                    act.wait_ge(cross_ready[h], k + 1)
                    chained(act, step, nc.scalar.activation(root[:, h], radicand[:, h], ACT.Ln, bias=mem.tiny_log[:]))
                    nc.scalar.activation(root[:, h], root[:, h], ACT.Exp, scale=0.5).then_inc(root_ready[h], 1)
                    nc.scalar.activation(half_cross[:, h], cross[:, h], ACT.Copy, scale=0.5)
                    act.wait_ge(sum_ready[h], k + 1)
                    chained(act, step, nc.scalar.activation(inverse[:, h], root[:, h], ACT.Ln))
                    nc.scalar.activation(inverse[:, h], inverse[:, h], ACT.Exp, scale=-1.0).then_inc(inverse_ready[h], 1)
                    act.wait_ge(sec_ready[h], k + 1)
                    chained(act, step, nc.scalar.activation(cosine[:, h], secant[:, h], ACT.Ln))
                    nc.scalar.activation(cosine[:, h], cosine[:, h], ACT.Exp, scale=-1.0).then_inc(cos_ready[h], 1)
                    if h == 1:
                        put_rotated(k, 0, dst)
                    elif not first:
                        put_rotated(k - 1, 1, src)
                    act.wait_ge(moved_ready[h], k + 1)
                    now = moved[:, h].rearrange("p k m (s j) -> p (k m) s j", s=2)
                    then = mem.weights[:, h].rearrange("p k m c -> p (k m) c")
                    for n, (to, a) in enumerate(places(now, then)):
                        if n == 0:
                            to = to.rearrange("p m (s j) -> p m s j", s=2)
                        last = nc.scalar.activation(to, a, ACT.Copy)
                    last.then_inc(weights_ready[h], 1)

            nc.scalar.preload_act_table_set("natural_log_exp_and_others")
            with act.Fori(0, SWEEPS) as sw:
                k0 = sw * ROUNDS
                round_(k0, mem.even, mem.odd, first=True)
                with act.Fori(0, ROUNDS // 2) as i:
                    round_(k0 + i * 2 + 1, mem.odd, mem.even)
                    round_(k0 + i * 2 + 2, mem.even, mem.odd)
                put_rotated(k0 + ROUNDS - 1, 1, mem.odd)
                for h in range(2):
                    act.wait_ge(weights_ready[h], (sw + 1) * ROUNDS)
                    nc.scalar.activation(scale[:, h], mem.weights[:, h, 1], ACT.Ln).then_inc(scale_log, 1)
                    act.wait_ge(scale_log, sw * 2 + h + 1)
                    nc.scalar.activation(scale[:, h], scale[:, h], ACT.Exp, scale=0.5).then_inc(scale_ready, 1)
                column_norms(nc, mem, norm_sems, sw)[0](act, scaled, (sw * 2 + 1, sw * 2 + 2), norms_ready)

        @block.gpsimd
        def _(pool):
            def round_(k):
                step = Count(pool_step, k * POOL_STEPS)
                for h in range(2):
                    w = mem.weights[:, h, 1].rearrange("p m (s j) -> p m s j", s=2)
                    norm = mem.weights[:, h, 0].rearrange("p m (s j) -> p m s j", s=2)
                    nc.gpsimd.tensor_tensor(gap[:, h], norm[:, :, 1], norm[:, :, 0], ALU.subtract).then_inc(gap_ready[h], 1)
                    hold(pool, dot_read[h], k + 1)
                    chained(pool, step, nc.gpsimd.tensor_tensor(weighed[:, h], swapped(w), over_sides(twice_dot[:, h]),
                                                                ALU.mult))
                    chained(pool, step, nc.gpsimd.tensor_tensor(cross[:, h], weighed[:, h, :, 0], weighed[:, h, :, 1],
                                                                ALU.mult))
                    nc.gpsimd.tensor_tensor(radicand[:, h], radicand[:, h], cross[:, h], ALU.add).then_inc(cross_ready[h], 1)
                    hold(pool, root_ready[h], k + 1)
                    nc.gpsimd.tensor_tensor(root[:, h], root[:, h], gap_abs[:, h], ALU.add).then_inc(sum_ready[h], 1)
                    hold(pool, inverse_ready[h], k + 1)
                    chained(pool, step, nc.gpsimd.tensor_tensor(ratio[:, h], twice(inverse[:, h]), gap_sign[:, h], ALU.mult))
                    by_pair = ratio[:, h].rearrange("p s m j -> p m s j")
                    nc.gpsimd.tensor_tensor(coef[:, h], weighed[:, h], by_pair, ALU.mult).then_inc(coef_ready[h], 1)
                    hold(pool, coef_ready[h], k + 1)
                    chained(pool, step, nc.gpsimd.tensor_tensor(secant[:, h], coef[:, h, :, 0], coef[:, h, :, 1], ALU.mult))
                    nc.gpsimd.tensor_tensor(secant[:, h], mem.one[:], secant[:, h], ALU.subtract).then_inc(sec_ready[h], 1)
                    mv = moved[:, h].rearrange("p k m (s j) -> p k m s j", s=2)
                    chained(pool, step, nc.gpsimd.tensor_tensor(mv[:, 0], over_sides(half_cross[:, h]), by_pair, ALU.mult))
                    step.up(nc.gpsimd.tensor_tensor(mv[:, 0], mv[:, 0], norm, ALU.add))
                    hold(pool, cos_ready[h], k + 1)
                    chained(pool, step, nc.gpsimd.tensor_tensor(secant[:, h], secant[:, h], cosine[:, h], ALU.mult))
                    chained(pool, step, nc.gpsimd.tensor_tensor(secant[:, h], mem.two[:], secant[:, h], ALU.subtract))
                    chained(pool, step, nc.gpsimd.tensor_tensor(cosine[:, h], cosine[:, h], secant[:, h], ALU.mult))
                    nc.gpsimd.tensor_tensor(mv[:, 1], w, over_sides(cosine[:, h]), ALU.mult).then_inc(moved_ready[h], 1)
                    hold(pool, weights_ready[h], k + 1)

            for h in range(2):
                nc.gpsimd.memset(mem.weights[:, h, 1], 1.0).then_inc(ones_ready, 1)
            pool.wait_ge(ones_ready, 2)
            with pool.Fori(0, SWEEPS) as sw:
                with pool.Fori(0, ROUNDS) as i:
                    round_(sw * ROUNDS + i)
                hold(pool, left_over, sw * 6 + 6)
                hold(pool, norms_ready, sw * 4 + 4)


def logarithm(nc, mem):
    with ExitStack() as ctx:
        def sem(name):
            return ctx.enter_context(nc.semaphore(name))

        def per_column(name):
            return ctx.enter_context(nc.sbuf_tensor(name, [P, 2, HB, S], F32))

        true_square, true_length, hat_length = (per_column(n) for n in ("true_square", "true_length", "hat_length"))
        height, root_height, spare = (per_column(n) for n in ("height", "root_height", "log_spare"))
        factor = ctx.enter_context(nc.sbuf_tensor("factor", [P, B, S], F32))
        banks = mem.banks
        spectrum, step = sem("spectrum"), sem("log_step")
        staged, turned, turned_out, formed = (sem(n) for n in ("log_staged", "log_turned", "log_turned_out", "log_formed"))
        formed_out = (sem("log_out_by_act"), sem("log_out_by_dve"))
        summed, averaged = sem("log_summed"), sem("log_averaged")
        stage = mem.product[0].rearrange("p (r q j) -> p r q j", q=4, j=S)
        tcol = mem.work[:, 1].rearrange("p (k r) -> p k r", r=S)
        logs = mem.odd[:].rearrange("p (a b) n -> p a (b n)", a=QUADS)
        hat_square, left_over = mem.weights[:, :, 0], mem.weights[:, :, 1]
        fac2 = factor[:].rearrange("p (h m) c -> p h m c", h=2)
        block = ctx.enter_context(nc.Block())

        @block.scalar
        def _(act):
            nc.scalar.activation(hat_length[:], hat_square, ACT.Sqrt)
            act.wait_ge(step, 1)
            nc.scalar.activation(true_length[:], true_square[:], ACT.Sqrt).then_inc(spectrum, 1)
            act.wait_ge(step, 11)
            nc.scalar.activation(height[:], true_length[:], ACT.Ln).then_inc(spectrum, 1)
            act.wait_ge(step, 13)
            nc.scalar.activation(root_height[:], height[:], ACT.Sqrt, bias=mem.tiny[:]).then_inc(spectrum, 1)
            with act.Fori(0, QUADS) as g:
                for b in range(8):
                    act.wait_ge(turned, g * 8 + b + 1)
                    nc.scalar.activation(tcol[:, :, 4 * b:4 * b + 4],
                                         banks[b % 4][:].rearrange("p (r k) -> p k r", r=4), ACT.Copy).then_inc(turned_out, 1)
                for b in range(0, 8, 2):
                    act.wait_ge(formed, g * 8 + b + 1)
                    nc.scalar.activation(logs[:, g, 512 * b:512 * b + 512], banks[4 + b % 4][:], ACT.Copy)\
                        .then_inc(formed_out[0], 1)

        @block.vector
        def _(dve):
            nc.vector.tensor_tensor(true_square[:], hat_square, left_over, ALU.mult).then_inc(step, 1)
            dve.wait_ge(spectrum, 1)
            refine_root(nc, dve, step, 1, hat_length[:], hat_square, spare[:])
            refine_root(nc, dve, step, 5, true_length[:], true_square[:], spare[:])
            sh = mem.shift[:].rearrange("p (h m n) -> p h m n", h=2, n=1).broadcast_to([P, 2, HB, S])
            nc.vector.tensor_tensor(true_length[:], true_length[:], sh, ALU.subtract).then_inc(step, 1)
            dve.wait_ge(step, 10)
            nc.vector.tensor_scalar(true_length[:], true_length[:], EPS_LOG, None, ALU.max).then_inc(step, 1)
            dve.wait_ge(spectrum, 2)
            nc.vector.tensor_scalar(height[:], height[:], -math.log(EPS_LOG), 0.0, ALU.add, ALU.max).then_inc(step, 1)
            nc.vector.reciprocal(hat_length[:], hat_length[:]).then_inc(step, 1)
            dve.wait_ge(spectrum, 3)
            refine_root(nc, dve, step, 13, root_height[:], height[:], spare[:])
            nc.vector.tensor_tensor(fac2, root_height[:], hat_length[:], ALU.mult).then_inc(step, 1)
            dve.wait_ge(step, 18)
            with dve.Fori(0, QUADS) as g:
                fb = factor[:, bass.ds(g * 4, 4), :].rearrange("p q (j r) -> p q j r", r=1).broadcast_to([P, 4, S, S])
                src = mem.even[:, bass.ds(g * 4, 4), :].rearrange("p q (j r) -> p q j r", r=S)
                nc.vector.tensor_tensor(stage.rearrange("p r q j -> p q j r"), src, fb, ALU.mult).then_inc(staged, 1)
                for b in range(1, 8, 2):
                    dve.wait_ge(formed, g * 8 + b + 1)
                    nc.vector.tensor_copy(logs[:, g, 512 * b:512 * b + 512], banks[4 + b % 4][:]).then_inc(formed_out[1], 1)
            for out in formed_out:
                dve.wait_ge(out, QUADS * 4)
            nc.vector.tensor_reduce(factor[:, 0, :], mem.odd[:].rearrange("p a (b n) -> p n (a b)", n=S), AX.X,
                                    ALU.add).then_inc(summed, 1)

        @block.tensor
        def _(pe):
            with pe.Fori(0, QUADS) as g:
                hold(pe, staged, g + 1)
                for b in range(8):
                    if b >= 4:
                        hold(pe, turned_out, g * 8 + b - 3)
                    for r in range(4):
                        last = nc.tensor.matmul(banks[b % 4][:, P * r:P * r + P],
                                                stage[:, 4 * b + r].rearrange("p q j -> p (q j)"), mem.ident[:],
                                                start=True, stop=True)
                    last.then_inc(turned, 1)
                hold(pe, turned_out, g * 8 + 8)
                for b in range(8):
                    if b >= 4:
                        hold(pe, formed_out[b % 2], g * 4 + (b - 4) // 2 + 1)
                    quad_products(nc, banks[4 + b % 4], tcol, tcol, 16 * b).then_inc(formed, 1)
                for out in formed_out:
                    hold(pe, out, g * 4 + 4)
            hold(pe, summed, 1)
            nc.tensor.matmul(banks[0][:, 0:S], mem.quad_mean[:], factor[:, 0, :], start=True, stop=True)\
                .then_inc(averaged, 1)

        @block.gpsimd
        def _(pool):
            hold(pool, averaged, 1)


def quad_products(nc, bank, left, right, first):
    for k in range(16):
        for q in range(4):
            rows = slice(S * q, S * q + S)
            last = nc.tensor.matmul(bank[rows, S * k:S * k + S], left[rows, first + k, :], right[rows, first + k, :],
                                    start=True, stop=True)
    return last


def exponential(nc, mem, gamma_dram, beta_dram):
    TM = 32
    W = TM * S
    TILES = B * N // W
    STEPS = 3 + SQUARINGS
    with ExitStack() as ctx:
        def sem(name):
            return ctx.enter_context(nc.semaphore(name))

        def tile(name):
            return ctx.enter_context(nc.sbuf_tensor(name, [P, TM, S], F32))

        a1, a2, a3, low, high = (tile(n) for n in ("a1", "a2", "a3", "low", "high"))
        power = [tile("power0"), tile("power1")]
        scal = ctx.enter_context(nc.sbuf_tensor("scal", [P, 4], F32))
        offset = ctx.enter_context(nc.sbuf_tensor("offset", [P, S], F32))
        eye = ctx.enter_context(nc.sbuf_tensor("eye", [P, 2, S], F32))
        loaded, step, eyes = sem("gb_loaded"), sem("exp_step"), sem("eyes")
        a_ready, product_done = sem("a_ready"), sem("product_done")
        copied = sem("copied")
        high_ready, low_ready = sem("high_ready"), sem("low_ready")
        banks = mem.banks
        logs = mem.odd[:].rearrange("p m n -> p (m n)")
        block = ctx.enter_context(nc.Block())
        c = TAYLOR

        def over(t):
            return t.rearrange("p (k c) -> p k c", k=1).broadcast_to([P, TM, S])

        @block.sync
        def _(sp):
            sp.dma_start(scal[:, 0:1], gamma_dram.partition_broadcast(P)).then_inc(loaded, 16)
            sp.dma_start(scal[:, 1:2], beta_dram.partition_broadcast(P)).then_inc(loaded, 16)

        @block.gpsimd
        def _(pool):
            for n, v in enumerate((c[0], c[3])):
                nc.gpsimd.memset(eye[:, n], 0.0).then_inc(eyes, 1)
            hold(pool, eyes, 2)
            n = 2
            for k, v in enumerate((c[0], c[3])):
                for q in range(4):
                    nc.gpsimd.affine_select(out=eye[:, k], in_=eye[:, k], compare_op=ALU.not_equal, fill=v,
                                            base=-S * q, pattern=[[-1, S]], channel_multiplier=1).then_inc(eyes, 1)
                    n += 1
                    hold(pool, eyes, n)

        @block.vector
        def _(dve):
            dve.wait_ge(loaded, 32)
            shrink = 2.0 ** -SQUARINGS
            nc.vector.tensor_scalar(scal[:, 2:3], scal[:, 0:1], -shrink, None, ALU.mult).then_inc(step, 1)
            nc.vector.tensor_scalar(scal[:, 3:4], scal[:, 1:2], shrink, None, ALU.mult).then_inc(step, 1)
            nc.vector.tensor_scalar(scal[:, 0:1], scal[:, 0:1], shrink, None, ALU.mult).then_inc(step, 1)
            dve.wait_ge(step, 3)
            nc.vector.tensor_scalar(offset[:], mem.banks[0][:, 0:S], scal[:, 2:3], scal[:, 3:4], ALU.mult, ALU.add)\
                .then_inc(step, 1)
            dve.wait_ge(step, 4)
            dve.wait_ge(eyes, 10)
            with dve.Fori(0, TILES) as t:
                k = Count(step, t * 2 + 4)
                nc.vector.scalar_tensor_tensor(a1[:], logs[:, bass.ds(t * W, W)].rearrange("p (k c) -> p k c", c=S),
                                               scal[:, 0:1], over(offset[:]), ALU.mult, ALU.add).then_inc(a_ready, 1)
                dve.wait_ge(a_ready, t + 1)
                nc.vector.scalar_tensor_tensor(low[:], a1[:], c[1], over(eye[:, 0]), ALU.mult, ALU.add)
                chained(dve, k, nc.vector.scalar_tensor_tensor(high[:], a1[:], c[4], over(eye[:, 1]), ALU.mult, ALU.add))
                dve.wait_ge(copied, t * (2 * STEPS) + 2)
                nc.vector.scalar_tensor_tensor(low[:], a2[:], c[2], low[:], ALU.mult, ALU.add)
                chained(dve, k, nc.vector.scalar_tensor_tensor(high[:], a2[:], c[5], high[:], ALU.mult, ALU.add))
                dve.wait_ge(copied, t * (2 * STEPS) + 4)
                nc.vector.scalar_tensor_tensor(high[:], a3[:], c[6], high[:], ALU.mult, ALU.add).then_inc(high_ready, 1)
                for g in range(2):
                    dve.wait_ge(product_done, t * (2 * STEPS) + 5 + g)
                    nc.vector.tensor_tensor(power[0][:, 16 * g:16 * g + 16, :],
                                            banks[4 + g][:].rearrange("p (k c) -> p k c", c=S),
                                            low[:, 16 * g:16 * g + 16, :], ALU.add).then_inc(low_ready, 1)

        @block.scalar
        def _(act):
            with act.Fori(0, TILES) as t:
                for n in range(STEPS):
                    if n == 2:
                        continue
                    dest = a2 if n == 0 else a3 if n == 1 else power[n % 2]
                    for g in range(2):
                        act.wait_ge(product_done, t * (2 * STEPS) + 2 * n + g + 1)
                        src = banks[2 * (n % 4) + g][:]
                        if n < STEPS - 1:
                            out = dest[:, 16 * g:16 * g + 16, :].rearrange("p k c -> p (k c)")
                        else:
                            out = logs[:, bass.ds(t * W + 512 * g, 512)]
                        nc.scalar.activation(out, src, ACT.Copy).then_inc(copied, 1)
                    if n == 1:
                        act.wait_ge(low_ready, t * 2 + 2)
                        for g in range(2):
                            nc.scalar.sem_inc(copied, 1)

        @block.tensor
        def _(pe):
            with pe.Fori(0, TILES) as t:
                for n in range(STEPS):
                    left, right = {0: (a1, a1), 1: (a1, a2), 2: (a3, high)}.get(n, (power[(n - 1) % 2],) * 2)
                    for g in range(2):
                        if n == 0:
                            hold(pe, a_ready, t + 1)
                        elif n == 2:
                            hold(pe, high_ready, t + 1)
                        else:
                            hold(pe, copied, t * (2 * STEPS) + 2 * (n - 1) + g + 1)
                        quad_products(nc, banks[2 * (n % 4) + g], left, right, 16 * g).then_inc(product_done, 1)


def back_to_channels(nc, mem, x_dram):
    with ExitStack() as ctx:
        def sem(name):
            return ctx.enter_context(nc.semaphore(name))

        loaded, staged, turned, added = sem("x_again"), sem("back_staged"), sem("back_turned"), sem("back_added")
        stage = [mem.work[:, n].rearrange("p (c k) -> p c k", k=P) for n in range(2)]
        powers = mem.odd[:].rearrange("p (g b) n -> p g (b n)", g=QUADS)
        banks = mem.banks
        block = ctx.enter_context(nc.Block())

        @block.sync
        def _(sp):
            sp.dma_start(mem.even[:], x_dram).then_inc(loaded, 16)

        @block.gpsimd
        def _(pool):
            hold(pool, loaded, 16)

        @block.scalar
        def _(act):
            with act.Fori(0, QUADS) as g:
                nc.scalar.activation(stage[0].rearrange("p c k -> p k c"),
                                     powers[:, g, :].rearrange("p (k c) -> p k c", c=S), ACT.Copy).then_inc(staged, 1)
                act.wait_ge(turned, g * 8 + 8)

        @block.tensor
        def _(pe):
            with pe.Fori(0, QUADS) as g:
                hold(pe, staged, g + 1)
                for b in range(8):
                    if b >= 4:
                        hold(pe, added, g * 8 + b - 3)
                    for n in range(4):
                        last = nc.tensor.matmul(banks[b % 4][:, P * n:P * n + P], stage[0][:, 4 * b + n, :], mem.ident[:],
                                                start=True, stop=True)
                    last.then_inc(turned, 1)
                hold(pe, added, g * 8 + 8)

        @block.vector
        def _(dve):
            dve.wait_ge(loaded, 16)
            with dve.Fori(0, QUADS) as g:
                for b in range(8):
                    dve.wait_ge(turned, g * 8 + b + 1)
                    d = mem.even[:, bass.ds(g * 4, 4), :].rearrange("p q (r c) -> p q r c", c=S)[:, :, :, 4 * b:4 * b + 4]
                    d = d.rearrange("p q r c -> p c q r")
                    nc.vector.tensor_tensor(d, d, banks[b % 4][:].rearrange("p (c q r) -> p c q r", c=4, q=4),
                                            ALU.add).then_inc(added, 1)


HEADS = 8
DH = P // HEADS
SLOT = 32
GROUPS = 2
QB = N // 2
KT = N // P
TOPK = 32
EXPERTS = 4
RANK = 16
LORA = EXPERTS * RANK
EPS_LN = 1e-5
OCTANTS = 8
MARGIN = 24.0
NEGATIVE = -3.0e38
PARTS_Q = [0, 0, 1, 1, 0, 2]
PARTS_K = [0, 1, 0, 1, 2, 0]
DEPTH = DH * len(PARTS_Q)
SHIFT_ROWS = 3
UNITS = 2 * GROUPS


class Tiles:

    def __init__(self, sb):
        self.wq = sb("w_wq", [P, P])
        self.wk = sb("w_wk", [P, P])
        self.wv = sb("w_wv", [P, P])
        self.wo = sb("w_wo", [P, GROUPS, P])
        self.bo = sb("w_bo", [P, 1])
        self.fc1t = sb("w_fc1t", [P, EXPERTS, P])
        self.lora_a = sb("w_lora_a", [P, EXPERTS, LORA])
        self.lora_out = sb("w_lora_out", [LORA, P])
        self.gates_t = sb("w_gates_t", [P, EXPERTS + 1])
        self.average = sb("w_average", [P, P])
        self.mean_column = sb("w_mean_column", [P, 1])
        self.select = sb("w_select", [P, P])
        self.stack_q = sb("w_stack_q", [P, HEADS, 3, DEPTH], BF16)
        self.stack_k = sb("w_stack_k", [P, HEADS, 3, DEPTH], BF16)
        self.ident = sb("w_ident", [P, P], BF16)
        self.minus = sb("w_minus", [P, 2, 16])
        self.shift = sb("w_shift", [P, 16, SHIFT_ROWS], BF16)
        self.centred = sb("w_centred", [P, N])
        self.squares = sb("w_squares", [P, N])
        self.z = sb("w_z", [P, N])
        self.t = sb("w_t", [P, N])
        self.var = sb("w_var", [P, KT])
        self.var_spare = sb("w_var_spare", [P, KT])
        self.root = sb("w_root", [P, KT])
        self.root_wide = sb("w_root_wide", [P, KT, P])
        self.parts = sb("w_parts", [P, 2, 3, N], BF16)
        self.q = sb("w_q", [P, HEADS, N], BF16)
        self.k = sb("w_k", [P, HEADS, N], BF16)
        self.v = sb("w_v", [P, KT, HEADS, SLOT])
        self.best = sb("w_best", [P, 16, OCTANTS, 8])
        self.top = sb("w_top", [P, 16])
        self.eighth = sb("w_eighth", [P, 16])
        self.widest = sb("w_widest", [P, 2, 16])
        self.o = sb("w_o", [P, QB])
        self.inverse = sb("w_inverse", [P, QB])
        self.att = sb("w_att", [P, GROUPS, N])
        self.hid = sb("w_hid", [P, 2 * EXPERTS, QB])
        self.low = sb("w_low", [LORA, 2, QB])
        self.gate = sb("w_gate", [P, KT, EXPERTS])
        self.threshold = sb("w_threshold", [P, KT])
        self.gate_sum = sb("w_gate_sum", [P, KT])
        self.gate_wide = sb("w_gate_wide", [P, KT, LORA])
        self.scores, self.rest, self.masked, turned = (self.hid[:, 2 * n:2 * n + 2, :].rearrange("p a n -> p (a n)")
                                                       for n in range(4))
        self.turned = turned.rearrange("p (k n) -> p k n", k=KT)
        self.eight = sb("w_eight", [P, TOPK // 8, 8])
        self.minus_top = sb("w_minus_top", [P, 1])
        self.exp = [sb(f"w_exp{n}", [P, QB]) for n in range(4)]


def load_weights(nc, mem, w, dram):
    with ExitStack() as ctx:
        def sem(name):
            return ctx.enter_context(nc.semaphore(name))

        cleared, loaded, turned, copied, selected = (sem(n) for n in ("w_cleared", "w_loaded", "w_turned", "w_copied",
                                                                      "w_selected"))
        gates = ctx.enter_context(nc.sbuf_tensor("gates", [EXPERTS + 1, P], F32))
        fc1, fc2, fc2t = (w.hid[:, n, :].rearrange("p (e i) -> p e i", e=EXPERTS) for n in range(3))
        lora_b = w.hid[0:RANK, 3, :].rearrange("r (e o) -> r e o", e=EXPERTS)
        lora_bt = w.hid[:, 4, 0:EXPERTS * LORA].rearrange("p (e r) -> p e r", e=EXPERTS)
        banks = mem.banks
        DMAS = 9 + HEADS + EXPERTS
        block = ctx.enter_context(nc.Block())
        pads = (w.wo[:], w.lora_a[:], lora_bt, w.select[:], w.stack_q[:], w.stack_k[:])

        @block.gpsimd
        def _(pool):
            for t in pads:
                nc.gpsimd.memset(t, 0.0).then_inc(cleared, 1)
            nc.gpsimd.memset(w.average[:], 1.0 / P)
            nc.gpsimd.memset(w.mean_column[:], 1.0 / P)
            nc.gpsimd.memset(w.widest[:], 0.0)
            nc.gpsimd.memset(w.v[:], 1.0).then_inc(cleared, 1)
            pool.wait_ge(cleared, len(pads) + 1)
            nc.gpsimd.memset(w.k[DEPTH:DEPTH + SHIFT_ROWS], 1.0).then_inc(cleared, 1)
            pool.wait_ge(cleared, len(pads) + 2)
            nc.gpsimd.affine_select(out=w.select[:].rearrange("p (j r) -> p j r", r=SLOT),
                                    in_=w.select[:].rearrange("p (j r) -> p j r", r=SLOT),
                                    compare_op=ALU.not_equal, fill=1.0, base=-DH, pattern=[[-SLOT, 4], [0, SLOT]],
                                    channel_multiplier=1).then_inc(selected, 1)
            n = 1
            for stack, parts in ((w.stack_q, PARTS_Q), (w.stack_k, PARTS_K)):
                for term, part in enumerate(parts):
                    to = stack[:, :, part, DH * term:DH * term + DH]
                    nc.gpsimd.affine_select(out=to, in_=to, compare_op=ALU.not_equal, fill=1.0, base=0,
                                            pattern=[[-DH, HEADS], [-1, DH]], channel_multiplier=1).then_inc(selected, 1)
                    n += 1
            pool.wait_ge(selected, n)
            nc.gpsimd.tensor_copy(w.ident[:], mem.ident[:]).then_inc(selected, 1)
            pool.wait_ge(selected, n + 1)

        @block.sync
        def _(sp):
            sp.wait_ge(cleared, len(pads) + 2)

            def load(out, in_):
                sp.dma_start(out, in_).then_inc(loaded, 16)

            load(w.wq[:], dram["wq"])
            load(w.wk[:], dram["wk"])
            load(w.wv[:], dram["wv"])
            for h in range(HEADS):
                j = h % 4
                load(w.wo[SLOT * j:SLOT * j + DH, h // 4, :], dram["wo"][DH * h:DH * h + DH, :])
            load(w.bo[:], dram["bo"].rearrange("(c n) -> c n", n=1))
            load(fc1, dram["fc1"].rearrange("e h i -> h e i"))
            load(fc2, dram["fc2"].rearrange("e d o -> d e o"))
            load(gates[0:EXPERTS, :], dram["gate"])
            load(gates[EXPERTS:EXPERTS + 1, :], dram["thr"])
            for e in range(EXPERTS):
                load(w.lora_a[:, e, RANK * e:RANK * e + RANK], dram["lora_a"][e])
            load(lora_b, dram["lora_b"].rearrange("e r o -> r e o"))
            sp.wait_ge(loaded, 16 * DMAS)

        @block.tensor
        def _(pe):
            pe.wait_ge(loaded, 16 * DMAS)
            for e in range(EXPERTS):
                nc.tensor.matmul(banks[0][:, P * e:P * e + P], fc1[:, e, :], mem.ident[:], start=True, stop=True)
                nc.tensor.matmul(banks[1][:, P * e:P * e + P], fc2[:, e, :], mem.ident[:], start=True, stop=True)
                nc.tensor.matmul(banks[2][:, RANK * e:RANK * e + RANK], lora_b[:, e, :], mem.ident[0:RANK, 0:RANK],
                                 start=True, stop=True)
            nc.tensor.matmul(banks[3][:, 0:EXPERTS + 1], gates[:], mem.ident[0:EXPERTS + 1, 0:EXPERTS + 1],
                             start=True, stop=True).then_inc(turned, 1)
            pe.wait_ge(copied, 1)
            for e in range(EXPERTS):
                last = nc.tensor.matmul(banks[4][0:LORA, 0:P], lora_bt[:, e, :], fc2t[:, e, :],
                                        start=(e == 0), stop=(e == EXPERTS - 1))
            last.then_inc(turned, 1)

        @block.vector
        def _(dve):
            dve.wait_ge(turned, 1)
            nc.vector.tensor_copy(w.fc1t[:].rearrange("p e n -> p (e n)"), banks[0][:])
            nc.vector.tensor_copy(w.hid[:, 2, :], banks[1][:])
            for e in range(EXPERTS):
                nc.vector.tensor_copy(lora_bt[:, e, RANK * e:RANK * e + RANK], banks[2][:, RANK * e:RANK * e + RANK])
            nc.vector.tensor_copy(w.gates_t[:], banks[3][:, 0:EXPERTS + 1]).then_inc(copied, 1)
            dve.wait_ge(turned, 2)
            nc.vector.tensor_copy(w.lora_out[:], banks[4][0:LORA, 0:P]).then_inc(copied, 1)


class PassSemaphores:

    def __init__(self, sem):
        self.averaged = sem("averaged")
        self.centred = sem("centred")
        self.squared = sem("squared")
        self.variances = sem("variances")
        self.spread_ready = sem("spread_ready")
        self.stats = sem("stats")
        self.rooted = sem("rooted")
        self.scale_spread = sem("scale_spread")
        self.normal = sem("normal")
        self.projected = sem("projected")
        self.first_parts = sem("first_parts")
        self.first_rests = sem("first_rests")
        self.second_parts = sem("second_parts")
        self.third_parts = sem("third_parts")
        self.stacked = sem("stacked")
        self.stack_out_act = sem("stack_out_act")
        self.stack_out_dve = sem("stack_out_dve")
        self.stack_out_late = sem("stack_out_late")
        self.v_out = sem("v_out")
        self.scored = sem("scored")
        self.read_max = sem("read_max")
        self.max_spread = sem("max_spread")
        self.max_turned = sem("max_turned")
        self.shifted = sem("shifted")
        self.scores_t = sem("scores_t")
        self.exp_done = sem("exp_done")
        self.weighed = sem("weighed")
        self.gathered = sem("gathered")
        self.den_spread = sem("den_spread")
        self.den_inverse = sem("den_inverse")
        self.inv_step = sem("inv_step")
        self.attended = sem("attended")
        self.joined = sem("joined")
        self.residual = sem("residual")
        self.gated = sem("gated")
        self.gate_exp = sem("gate_exp")
        self.gate_done = sem("gate_done")
        self.gates_t_done = sem("gates_t_done")
        self.hidden = sem("hidden")
        self.hidden_act = sem("hidden_act")
        self.hidden_dve = sem("hidden_dve")
        self.low = sem("low")
        self.low_out = sem("low_out")
        self.mixed = sem("mixed")
        self.mixed_low = sem("mixed_low")
        self.expert_out = sem("expert_out")
        self.finished = sem("finished")
        self.stored = sem("stored")
        self.dve_stats = sem("dve_stats")
        self.gate_steps = sem("gate_steps")
        self.maxima = sem("maxima")
        self.g_copied = sem("g_copied")
        self.g_ranked = sem("g_ranked")
        self.g_exp = sem("g_exp")
        self.g_masked = sem("g_masked")
        self.g_turned = sem("g_turned")
        self.g_turned_out = sem("g_turned_out")
        self.g_pv = sem("g_pv")
        self.rank_steps = sem("rank_steps")


def image_pass(nc, mem, w, s, out_dram, general):
    banks = mem.banks
    first = B if general else 0

    def tokens(b):
        return mem.even[:, bass.ds(b - first, 1), :].rearrange("p m n -> p (m n)")

    def norm_pe(pe, n, source):
        for k in range(2):
            last = nc.tensor.matmul(banks[k][:], w.average[:], source[:, QB * k:QB * k + QB], start=True, stop=True)
        last.then_inc(s.averaged, 1)
        hold(pe, s.squared, n + 1)
        for t in range(KT):
            last = nc.tensor.matmul(banks[2][:, t:t + 1], w.squares[:, P * t:P * t + P], w.mean_column[:],
                                    start=True, stop=True)
        last.then_inc(s.variances, 1)
        hold(pe, s.spread_ready, n + 1)
        for t in range(KT):
            last = nc.tensor.matmul(banks[t // 4][:, P * (t % 4):P * (t % 4) + P],
                                    w.root_wide[:, t, :], mem.ident[:], start=True, stop=True)
        last.then_inc(s.scale_spread, 1)

    def norm_act(act, n):
        act.wait_ge(s.centred, n + 1)
        nc.scalar.activation(w.squares[:], w.centred[:], ACT.Square).then_inc(s.squared, 1)
        act.wait_ge(s.stats, n + 1)
        nc.scalar.activation(w.root[:], w.var[:], ACT.Ln).then_inc(s.rooted, 1)
        act.wait_ge(s.rooted, n * 2 + 1)
        nc.scalar.activation(w.root[:], w.root[:], ACT.Exp, scale=0.5).then_inc(s.rooted, 1)

    def norm_dve(dve, n, source, result):
        dve.wait_ge(s.averaged, n + 1)
        for k in range(2):
            last = nc.vector.tensor_tensor(w.centred[:, QB * k:QB * k + QB], source[:, QB * k:QB * k + QB], banks[k][:],
                                           ALU.subtract)
        last.then_inc(s.centred, 1)
        dve.wait_ge(s.variances, n + 1)
        nc.vector.tensor_scalar(w.var[:], banks[2][:, 0:KT], EPS_LN, None, ALU.add).then_inc(s.stats, 1)
        dve.wait_ge(s.rooted, n * 2 + 2)
        refine_root(nc, dve, s.dve_stats, n * 5, w.root[:], w.var[:], w.var_spare[:])
        nc.vector.reciprocal(w.root[:], w.root[:]).then_inc(s.dve_stats, 1)
        dve.wait_ge(s.dve_stats, n * 5 + 5)
        nc.vector.tensor_copy(w.root_wide[:], w.root[:].rearrange("p (t n) -> p t n", n=1).broadcast_to([P, KT, P]))\
            .then_inc(s.spread_ready, 1)
        dve.wait_ge(s.scale_spread, n + 1)
        for k in range(2):
            last = nc.vector.tensor_tensor(result[:, QB * k:QB * k + QB], w.centred[:, QB * k:QB * k + QB], banks[k][:],
                                           ALU.mult)
        last.then_inc(s.normal, 1)

    CHUNKS = 2 * HEADS * 2
    EARLY = CHUNKS // GROUPS
    STACK_BANKS = (6, 7, 4, 5)

    def chunk(c):
        return c // 8 % 2, 4 * (c // EARLY) + c // 2 % 4, c % 2

    def stack_pe(c):
        which, h, k = chunk(c)
        stack = (w.stack_q, w.stack_k)[which]
        for part in range(3):
            last = nc.tensor.matmul(banks[STACK_BANKS[c % 4]][0:DEPTH, :], stack[:, h, part, :],
                                    w.parts[:, which, part, QB * k:QB * k + QB], start=(part == 0), stop=(part == 2))
        last.then_inc(s.stacked, 1)

    def stack_late_pe(pe, b, n):
        if n >= 4:
            hold(pe, s.stack_out_late, b * (CHUNKS - EARLY) + n - 3)
        stack_pe(EARLY + n)

    def stack_late_act(act, b):
        for n in range(CHUNKS - EARLY):
            act.wait_ge(s.stacked, b * CHUNKS + EARLY + n + 1)
            nc.scalar.activation(stack_to(EARLY + n), banks[STACK_BANKS[n % 4]][0:DEPTH, :], ACT.Copy)\
                .then_inc(s.stack_out_late, 1)

    def project_pe(pe, b):
        hold(pe, s.normal, b * 2 + 1)
        for weight, first_bank in ((w.wq, 0), (w.wk, 2)):
            for k in range(2):
                last = nc.tensor.matmul(banks[first_bank + k][:], weight[:], w.z[:, QB * k:QB * k + QB],
                                        start=True, stop=True)
            last.then_inc(s.projected, 1)
        for t in range(KT):
            last = nc.tensor.matmul(banks[4 + t // 4][:, P * (t % 4):P * (t % 4) + P], w.z[:, P * t:P * t + P], w.wv[:],
                                    start=True, stop=True)
        last.then_inc(s.projected, 1)
        for c in range(EARLY):
            if c == 0:
                hold(pe, s.third_parts, b * 4 + 2)
            if c == 8:
                hold(pe, s.third_parts, b * 4 + 4)
            if c == 2:
                hold(pe, s.v_out, b + 1)
            if c >= 4:
                hold(pe, (s.stack_out_act, s.stack_out_dve)[c % 2], b * 8 + (c - 4) // 2 + 1)
            stack_pe(c)
        for out in (s.stack_out_act, s.stack_out_dve):
            hold(pe, out, b * 8 + 8)

    def rests(c):
        return w.att[:, c // 2, QB * (c % 2):QB * (c % 2) + QB]

    def part_of(c, part):
        return w.parts[:, c // 2, part, QB * (c % 2):QB * (c % 2) + QB]

    def stack_to(c):
        which, h, k = chunk(c)
        return (w.q, w.k)[which][0:DEPTH, h, QB * k:QB * k + QB]

    def factor_of(c):
        return float(DH) ** -0.5 if c < 2 else 1.0

    def project_act(act, b):
        for c in range(4):
            act.wait_ge(s.projected, b * 3 + c // 2 + 1)
            nc.scalar.activation(part_of(c, 0), banks[c][:], ACT.Copy, scale=factor_of(c)).then_inc(s.first_parts, 1)
        for c in range(4):
            act.wait_ge(s.first_rests, b * 4 + c + 1)
            nc.scalar.activation(part_of(c, 1), rests(c), ACT.Copy).then_inc(s.second_parts, 1)
        act.wait_ge(s.projected, b * 3 + 3)
        for n in range(2):
            last = nc.scalar.activation(w.v[:, 4 * n:4 * n + 4, :, 0:DH],
                                        banks[4 + n][:].rearrange("p (t h d) -> p t h d", t=4, d=DH), ACT.Copy)
        last.then_inc(s.v_out, 1)
        for c in range(0, EARLY, 2):
            act.wait_ge(s.stacked, b * CHUNKS + c + 1)
            nc.scalar.activation(stack_to(c), banks[STACK_BANKS[c % 4]][0:DEPTH, :], ACT.Copy).then_inc(s.stack_out_act, 1)

    def project_dve(dve, b):
        for c in range(4):
            dve.wait_ge(s.first_parts, b * 4 + c + 1)
            nc.vector.scalar_tensor_tensor(rests(c), banks[c][:], factor_of(c), part_of(c, 0), ALU.mult, ALU.subtract)\
                .then_inc(s.first_rests, 1)
        for c in range(4):
            dve.wait_ge(s.second_parts, b * 4 + c + 1)
            nc.vector.tensor_tensor(part_of(c, 2), rests(c), part_of(c, 1), ALU.subtract).then_inc(s.third_parts, 1)
        for c in range(1, EARLY, 2):
            dve.wait_ge(s.stacked, b * CHUNKS + c + 1)
            nc.vector.tensor_copy(stack_to(c), banks[STACK_BANKS[c % 4]][0:DEPTH, :]).then_inc(s.stack_out_dve, 1)

    def slot(j):
        return slice(SLOT * j, SLOT * j + SLOT)

    def where(u):
        return u // 2, u % 2

    def score_pe(pe, b, u, i):
        g, qb = where(u)
        t, j = i // 4, i % 4
        q0 = QB * qb + P * t
        for k in range(2):
            last = nc.tensor.matmul(banks[2 * (i % 2) + k][:], w.q[0:DEPTH, 4 * g + j, q0:q0 + P],
                                    w.k[0:DEPTH, 4 * g + j, QB * k:QB * k + QB], start=True, stop=True)
        last.then_inc(s.scored, 1)

    def fast_pe(pe, b):
        base = b * UNITS
        for u in range(UNITS + 1):
            for i in range(16):
                if u < UNITS:
                    n = 16 * u + i
                    if i >= 2:
                        hold(pe, s.read_max, b * 64 + n - 1)
                    elif i == 0 and u >= 1:
                        hold(pe, s.shifted, base + u)
                    score_pe(pe, b, u, i)
                if u == 0:
                    stack_late_pe(pe, b, i)
                if u >= 1:
                    g, qb = where(u - 1)
                    if u == UNITS and i == 0:
                        hold(pe, s.shifted, base + u)
                    for x in range(2 * i, 2 * i + 2):
                        kt, j = x // 4, x % 4
                        m = 32 * (u - 1) + x
                        if m >= 3:
                            hold(pe, s.exp_done, b * 128 + m - 2)
                        nc.tensor.matmul(banks[4 + m % 3][:], w.k[0:DEPTH + SHIFT_ROWS, 4 * g + j, P * kt:P * kt + P],
                                         w.q[0:DEPTH + SHIFT_ROWS, 4 * g + j, QB * qb:QB * qb + QB],
                                         start=True, stop=True)\
                            .then_inc(s.scores_t, 1)
                        if x >= 2:
                            weigh_pe(pe, b, u - 1, x - 2)
            if u >= 1:
                weigh_pe(pe, b, u - 1, 30)
                weigh_pe(pe, b, u - 1, 31)
                finish_pe(pe, base + u - 1)
            if u == 0:
                hold(pe, s.stack_out_late, (b + 1) * (CHUNKS - EARLY))
            if u < UNITS:
                hold(pe, s.max_spread, base + u + 1)
                for i in range(16):
                    t, j = i // 4, i % 4
                    last = nc.tensor.matmul(banks[j][DEPTH:DEPTH + SHIFT_ROWS, P * t:P * t + P], w.shift[:, i, :],
                                            w.ident[:], start=True, stop=True)
                last.then_inc(s.max_turned, 1)

    def weigh_pe(pe, b, u, x):
        g, _ = where(u)
        kt, j = x // 4, x % 4
        m = 32 * u + x
        hold(pe, s.exp_done, b * 128 + m + 1)
        if x == 0 and u >= 1:
            hold(pe, s.den_inverse, b * UNITS + u)
        nc.tensor.matmul(banks[7][slot(j), :], w.v[:, kt, 4 * g + j, :], w.exp[m % 4][:], start=(kt == 0),
                         stop=(kt == KT - 1)).then_inc(s.weighed, 1)

    def finish_pe(pe, n):
        hold(pe, s.gathered, n + 1)
        nc.tensor.matmul(banks[7][:], w.select[:], w.o[:], start=True, stop=True).then_inc(s.den_spread, 1)

    def finish_act(act, n, done, done_at):
        act.wait_ge(done, done_at)
        nc.scalar.activation(w.o[:], banks[7][:], ACT.Copy).then_inc(s.gathered, 1)
        act.wait_ge(s.den_spread, n + 1)
        nc.scalar.activation(w.inverse[:], banks[7][:], ACT.Ln).then_inc(s.inv_step, 1)
        act.wait_ge(s.inv_step, n + 1)
        nc.scalar.activation(w.inverse[:], w.inverse[:], ACT.Exp, scale=-1.0).then_inc(s.den_inverse, 1)

    def finish_dve(dve, b, u):
        g, qb = where(u)
        dve.wait_ge(s.den_inverse, b * UNITS + u + 1)
        nc.vector.tensor_tensor(w.att[:, g, QB * qb:QB * qb + QB], w.o[:], w.inverse[:], ALU.mult).then_inc(s.attended, 1)

    def fast_act(act, b):
        stack_late_act(act, b)
        shift_act(act, b, 0)
        for u in range(UNITS):
            for x in range(32):
                m = 32 * u + x
                act.wait_ge(s.scores_t, b * 128 + m + 1)
                if m >= 4:
                    act.wait_ge(s.weighed, b * 128 + m - 3)
                nc.scalar.activation(w.exp[m % 4][:], banks[4 + m % 3][:], ACT.Exp).then_inc(s.exp_done, 1)
            if u >= 1:
                act.wait_ge(s.attended, b * UNITS + u)
            finish_act(act, b * UNITS + u, s.weighed, b * 128 + 32 * u + 32)
            if u + 1 < UNITS:
                shift_act(act, b, u + 1)

    def shift_act(act, b, u):
        g, qb = where(u)
        act.wait_ge(s.max_turned, b * UNITS + u + 1)
        for j in range(4):
            last = nc.scalar.activation(w.q[DEPTH:DEPTH + SHIFT_ROWS, 4 * g + j, QB * qb:QB * qb + QB],
                                        banks[j][DEPTH:DEPTH + SHIFT_ROWS, :], ACT.Copy)
        last.then_inc(s.shifted, 1)

    def fast_dve(dve, b):
        for u in range(UNITS):
            g, qb = where(u)
            for i in range(16):
                hold(dve, s.scored, b * 64 + 16 * u + i + 1)
                for o in range(OCTANTS):
                    last = nc.vector.max(w.best[:, i, o, :], banks[2 * (i % 2) + o // 4][:, P * (o % 4):P * (o % 4) + P])
                last.then_inc(s.read_max, 1)
            dve.wait_ge(s.read_max, b * 64 + 16 * u + 16)
            k = Count(s.maxima, (b * UNITS + u) * 12)
            chained(dve, k, nc.vector.tensor_reduce(w.top[:], w.best[:, :, :, 0], AX.X, ALU.max))
            rest, part = w.minus, w.shift
            chained(dve, k, nc.vector.tensor_scalar(rest[:, 0], w.top[:], -1.0, None, ALU.mult))
            chained(dve, k, nc.vector.tensor_copy(part[:, :, 0], rest[:, 0]))
            chained(dve, k, nc.vector.tensor_tensor(rest[:, 1], rest[:, 0], part[:, :, 0], ALU.subtract))
            chained(dve, k, nc.vector.tensor_copy(part[:, :, 1], rest[:, 1]))
            nc.vector.tensor_tensor(part[:, :, 2], rest[:, 1], part[:, :, 1], ALU.subtract).then_inc(s.max_spread, 1)
            chained(dve, k, nc.vector.tensor_reduce(w.eighth[:], w.best[:, :, :, 7], AX.X, ALU.max))
            k.up(nc.vector.tensor_tensor(w.eighth[:], w.eighth[:], w.top[:], ALU.subtract))
            chained(dve, k, nc.vector.tensor_scalar(w.top[:], w.top[:], -MARGIN, None, ALU.add))
            k.up(nc.vector.scalar_tensor_tensor(w.widest[:, 0], w.eighth[:], MARGIN, w.widest[:, 0], ALU.add, ALU.max))
            near = w.best[:].rearrange("p i o e -> p i (o e)")
            chained(dve, k, nc.vector.tensor_tensor(near, near, w.top[:].rearrange("p (i n) -> p i n", n=1)
                                                    .broadcast_to([P, 16, 8 * OCTANTS]), ALU.is_gt))
            chained(dve, k, nc.vector.tensor_reduce(w.eighth[:], near, AX.X, ALU.add))
            chained(dve, k, nc.vector.scalar_tensor_tensor(w.widest[:, 1], w.eighth[:], -float(TOPK), w.widest[:, 1],
                                                           ALU.add, ALU.max))
            if u >= 1:
                finish_dve(dve, b, u - 1)
        finish_dve(dve, b, UNITS - 1)

    def general_pe(pe, b):
        for n in range(CHUNKS - EARLY):
            stack_late_pe(pe, b, n)
        hold(pe, s.stack_out_late, (b + 1) * (CHUNKS - EARLY))
        for u in range(UNITS):
            g, _ = where(u)
            for i in range(16):
                n = 16 * u + i
                if n >= 2:
                    hold(pe, s.g_copied, (b - first) * 64 + n - 1)
                score_pe(pe, b, u, i)
                hold(pe, s.g_masked, (b - first) * 64 + n + 1)
                if n >= 1:
                    hold(pe, s.g_turned_out, (b - first) * 64 + n)
                for kt in range(KT):
                    last = nc.tensor.matmul(banks[4 + kt // 4][:, P * (kt % 4):P * (kt % 4) + P],
                                            w.masked[:, P * kt:P * kt + P], mem.ident[:], start=True, stop=True)
                last.then_inc(s.g_turned, 1)
                hold(pe, s.g_turned_out, (b - first) * 64 + n + 1)
                if i == 0 and u >= 1:
                    hold(pe, s.den_inverse, b * UNITS + u)
                t, j = i // 4, i % 4
                for kt in range(KT):
                    last = nc.tensor.matmul(banks[7][slot(j), P * t:P * t + P], w.v[:, kt, 4 * g + j, :],
                                            w.turned[:, kt, :], start=(kt == 0), stop=(kt == KT - 1))
                last.then_inc(s.g_pv, 1)
            finish_pe(pe, b * UNITS + u)

    def general_act(act, b):
        stack_late_act(act, b)
        for u in range(UNITS):
            for i in range(16):
                n = 16 * u + i
                act.wait_ge(s.scored, b * 64 + n + 1)
                for k in range(2):
                    last = nc.scalar.activation(w.scores[:, QB * k:QB * k + QB], banks[2 * (i % 2) + k][:], ACT.Copy)
                last.then_inc(s.g_copied, 1)
                act.wait_ge(s.g_ranked, (b - first) * 64 + n + 1)
                nc.scalar.activation(w.masked, w.scores, ACT.Exp, bias=w.minus_top[:]).then_inc(s.g_exp, 1)
                act.wait_ge(s.g_turned, (b - first) * 64 + n + 1)
                if n >= 1:
                    act.wait_ge(s.g_pv, (b - first) * 64 + n)
                for k in range(2):
                    last = nc.scalar.activation(w.turned[:, 4 * k:4 * k + 4, :].rearrange("p k n -> p (k n)"),
                                                banks[4 + k][:], ACT.Copy)
                last.then_inc(s.g_turned_out, 1)
            if u >= 1:
                act.wait_ge(s.attended, b * UNITS + u)
            finish_act(act, b * UNITS + u, s.g_pv, (b - first) * 64 + 16 * u + 16)

    def general_dve(dve, b):
        for u in range(UNITS):
            for i in range(16):
                n = 16 * u + i
                hold(dve, s.g_copied, (b - first) * 64 + n + 1)
                k = Count(s.rank_steps, ((b - first) * 64 + n) * 8)
                source = w.scores
                for r in range(TOPK // 8):
                    chained(dve, k, nc.vector.max(w.eight[:, r, :], source))
                    chained(dve, k, nc.vector.match_replace(w.rest, w.eight[:, r, :], source, NEGATIVE))
                    source = w.rest
                nc.vector.tensor_scalar(w.minus_top[:], w.eight[:, 0, 0:1], -1.0, None, ALU.mult).then_inc(s.g_ranked, 1)
                dve.wait_ge(s.g_exp, (b - first) * 64 + n + 1)
                nc.vector.scalar_tensor_tensor(w.masked, w.rest, NEGATIVE, w.masked, ALU.is_equal, ALU.mult)\
                    .then_inc(s.g_masked, 1)
            finish_dve(dve, b, u)

    def join_pe(pe, b):
        hold(pe, s.attended, (b + 1) * UNITS)
        for k in range(2):
            for g in range(GROUPS):
                last = nc.tensor.matmul(banks[4 + k][:], w.wo[:, g, :], w.att[:, g, QB * k:QB * k + QB],
                                        start=(g == 0), stop=(g == GROUPS - 1))
        last.then_inc(s.joined, 1)

    def join_dve(dve, b):
        dve.wait_ge(s.joined, b + 1)
        hold(dve, s.stored, (b + 1) * 16)
        for k in range(2):
            part = slice(QB * k, QB * k + QB)
            last = nc.vector.scalar_tensor_tensor(w.t[:, part], banks[4 + k][:], w.bo[:], tokens(b)[:, part],
                                                  ALU.add, ALU.add)
        last.then_inc(s.residual, 1)

    def experts_pe(pe, b):
        hold(pe, s.normal, b * 2 + 2)
        for t in range(KT):
            last = nc.tensor.matmul(banks[2][:, 8 * t:8 * t + EXPERTS + 1], w.z[:, P * t:P * t + P], w.gates_t[:],
                                    start=True, stop=True)
        last.then_inc(s.gated, 1)
        n = 0
        for k in range(2):
            for e in range(EXPERTS):
                if n >= 2:
                    out = s.hidden_act if n % 2 == 0 else s.hidden_dve
                    hold(pe, out, b * 4 + n // 2)
                nc.tensor.matmul(banks[n % 2][:], w.fc1t[:, e, :], w.z[:, QB * k:QB * k + QB], start=True, stop=True)\
                    .then_inc(s.hidden, 1)
                n += 1
        for k in range(2):
            for e in range(EXPERTS):
                n = EXPERTS * k + e
                hold(pe, s.hidden_act if n % 2 == 0 else s.hidden_dve, b * 4 + n // 2 + 1)
                last = nc.tensor.matmul(banks[4 + k][0:LORA, :], w.lora_a[:, e, :], w.hid[:, n, :],
                                        start=(e == 0), stop=(e == EXPERTS - 1))
            last.then_inc(s.low, 1)
        hold(pe, s.gate_done, b + 1)
        for t in range(KT):
            last = nc.tensor.matmul(banks[6 + t // 4][0:LORA, P * (t % 4):P * (t % 4) + P], w.gate_wide[:, t, :],
                                    mem.ident[:], start=True, stop=True)
        last.then_inc(s.gates_t_done, 1)
        hold(pe, s.mixed_low, b + 1)
        for k in range(2):
            last = nc.tensor.matmul(banks[k][:], w.lora_out[:], w.low[:, k, :], start=True, stop=True)
        last.then_inc(s.expert_out, 1)

    def experts_act(act, b):
        act.wait_ge(s.gated, b + 1)
        act.wait_ge(s.gate_steps, b * GATE_STEPS + 3)
        nc.scalar.activation(w.gate[:, :, 0:EXPERTS], w.gate[:, :, 0:EXPERTS], ACT.Exp)
        nc.scalar.activation(w.threshold[:], w.threshold[:], ACT.Exp, scale=-1.0).then_inc(s.gate_exp, 1)
        for n in range(0, 2 * EXPERTS, 2):
            act.wait_ge(s.hidden, b * 8 + n + 1)
            nc.scalar.activation(w.hid[:, n, :], banks[0][:], ACT.Relu).then_inc(s.hidden_act, 1)
        for k in range(2):
            act.wait_ge(s.low, b * 2 + k + 1)
            last = nc.scalar.activation(w.low[:, k, :], banks[4 + k][0:LORA, :], ACT.Copy)
        last.then_inc(s.low_out, 1)

    GATE_STEPS = 13

    def experts_dve(dve, b):
        k = Count(s.gate_steps, b * GATE_STEPS)
        gate = w.gate[:, :, 0:EXPERTS]
        logits = banks[2][:, 0:8 * KT].rearrange("p (t x) -> p t x", x=8)[:, :, 0:EXPERTS]

        def over(t):
            return t.rearrange("p (t n) -> p t n", n=1).broadcast_to([P, KT, EXPERTS])

        dve.wait_ge(s.gated, b + 1)
        k.up(nc.vector.tensor_scalar(w.threshold[:], banks[2][:, 0:8 * KT].rearrange("p (t x) -> p t x", x=8)[:, :, EXPERTS],
                                     -87.0, None, ALU.max))
        chained(dve, k, nc.vector.tensor_reduce(w.gate_sum[:], logits, AX.X, ALU.max))
        chained(dve, k, nc.vector.tensor_tensor(gate, logits, over(w.gate_sum[:]), ALU.subtract))
        for n in range(1, 2 * EXPERTS, 2):
            dve.wait_ge(s.hidden, b * 8 + n + 1)
            nc.vector.tensor_scalar(w.hid[:, n, :], banks[1][:], 0.0, None, ALU.max).then_inc(s.hidden_dve, 1)
        dve.wait_ge(s.gate_exp, b + 1)
        k.up(nc.vector.tensor_scalar(w.threshold[:], w.threshold[:], 1.0, float(EXPERTS), ALU.add, ALU.mult))
        chained(dve, k, nc.vector.tensor_reduce(w.gate_sum[:], gate, AX.X, ALU.add))
        k.up(nc.vector.reciprocal(w.threshold[:], w.threshold[:]))
        chained(dve, k, nc.vector.reciprocal(w.gate_sum[:], w.gate_sum[:]))
        chained(dve, k, nc.vector.tensor_tensor(gate, gate, over(w.gate_sum[:]), ALU.mult))
        chained(dve, k, nc.vector.tensor_tensor(gate, gate, over(w.threshold[:]), ALU.subtract))
        chained(dve, k, nc.vector.tensor_scalar(gate, gate, 0.0, None, ALU.max))
        chained(dve, k, nc.vector.tensor_reduce(w.gate_sum[:], gate, AX.X, ALU.add))
        chained(dve, k, nc.vector.scalar_tensor_tensor(w.gate_sum[:], w.gate_sum[:], 0.0, w.gate_sum[:], ALU.is_equal,
                                                       ALU.add))
        chained(dve, k, nc.vector.reciprocal(w.gate_sum[:], w.gate_sum[:]))
        nc.vector.tensor_tensor(gate, gate, over(w.gate_sum[:]), ALU.mult).then_inc(s.mixed, 1)
        dve.wait_ge(s.mixed, b + 1)
        nc.vector.tensor_copy(w.gate_wide[:].rearrange("p t (e r) -> p t e r", r=RANK),
                              w.gate[:, :, 0:EXPERTS].rearrange("p t (e n) -> p t e n", n=1)
                              .broadcast_to([P, KT, EXPERTS, RANK])).then_inc(s.gate_done, 1)
        dve.wait_ge(s.low_out, b + 1)
        dve.wait_ge(s.gates_t_done, b + 1)
        for n in range(2):
            last = nc.vector.tensor_tensor(w.low[:, n, :], w.low[:, n, :], banks[6 + n][0:LORA, :], ALU.mult)
        last.then_inc(s.mixed_low, 1)
        dve.wait_ge(s.expert_out, b + 1)
        for n in range(2):
            part = slice(QB * n, QB * n + QB)
            last = nc.vector.tensor_tensor(w.t[:, part], w.t[:, part], banks[n][:], ALU.add)
        last.then_inc(s.finished, 1)

    def pe_image(pe, b):
        norm_pe(pe, b * 2, tokens(b))
        project_pe(pe, b)
        (general_pe if general else fast_pe)(pe, b)
        join_pe(pe, b)
        hold(pe, s.residual, b + 1)
        norm_pe(pe, b * 2 + 1, w.t)
        experts_pe(pe, b)
        hold(pe, s.finished, b + 1)

    def act_image(act, b):
        norm_act(act, b * 2)
        project_act(act, b)
        (general_act if general else fast_act)(act, b)
        norm_act(act, b * 2 + 1)
        experts_act(act, b)

    def dve_image(dve, b):
        norm_dve(dve, b * 2, tokens(b), w.z)
        project_dve(dve, b)
        (general_dve if general else fast_dve)(dve, b)
        join_dve(dve, b)
        norm_dve(dve, b * 2 + 1, w.t, w.z)
        experts_dve(dve, b)

    def sp_image(sp, b):
        sp.wait_ge(s.finished, b + 1)
        sp.dma_start(out_dram[:, bass.ds(b - first, 1), :], w.t[:].rearrange("p (m n) -> p m n", m=1)).then_inc(s.stored, 16)

    return pe_image, act_image, dve_image, sp_image


def attention_and_experts(nc, mem, w, out_dram):
    with ExitStack() as ctx:
        s = PassSemaphores(lambda name: ctx.enter_context(nc.semaphore(name)))
        usual, general = (image_pass(nc, mem, w, s, out_dram, which) for which in (False, True))
        widest_ready, widest_turned, flag_ready = (ctx.enter_context(nc.semaphore(n)) for n in
                                                   ("widest_ready", "widest_turned", "flag_ready"))
        block = ctx.enter_context(nc.Block())

        def once(eng, n):
            with eng.Fori(0, B) as b:
                usual[n](eng, b)

        def again(eng, n):
            eng.wait_ge(flag_ready, 1)
            flag = eng.value_load(mem.flag[0:1, 0:1], min_val=0, max_val=1)
            with eng.If(flag > 0):
                with eng.Fori(B, 2 * B) as b:
                    general[n](eng, b)
                if n == 3:
                    eng.wait_ge(s.stored, 16 * (2 * B + 1))

        @block.tensor
        def _(pe):
            once(pe, 0)
            pe.wait_ge(widest_ready, 1)
            nc.tensor.matmul(mem.banks[0][0:1, 0:P], w.top[:, 0:1], mem.ident[:], start=True, stop=True)\
                .then_inc(widest_turned, 1)
            again(pe, 0)

        @block.scalar
        def _(act):
            nc.scalar.preload_act_table_set("natural_log_exp_and_others")
            once(act, 1)
            again(act, 1)

        @block.vector
        def _(dve):
            once(dve, 2)
            nc.vector.tensor_reduce(w.top[:, 0:1], w.widest[:].rearrange("p a b -> p (a b)"), AX.X, ALU.max)\
                .then_inc(widest_ready, 1)
            dve.wait_ge(widest_turned, 1)
            nc.vector.tensor_reduce(w.eighth[0:1, 0:1], mem.banks[0][0:1, 0:P], AX.X, ALU.max).then_inc(widest_ready, 1)
            dve.wait_ge(widest_ready, 2)
            nc.vector.tensor_scalar(mem.flag[0:1, 0:1], w.eighth[0:1, 0:1], 0.0, None, ALU.is_gt).then_inc(flag_ready, 1)
            again(dve, 2)

        @block.sync
        def _(sp):
            sp.sem_inc(s.stored, 16)
            once(sp, 3)
            sp.wait_ge(s.stored, 16 * (B + 1))
            again(sp, 3)


def hybrid_kernel(nc, dram, out):
    x_dram = dram["x"].rearrange("b c h w -> c b (h w)")
    out_dram = out.rearrange("b c h w -> c b (h w)")
    with ExitStack() as ctx:
        mem = Memory()

        def sb(name, shape, dtype=F32):
            return ctx.enter_context(nc.sbuf_tensor(name, shape, dtype))

        mem.flag = ctx.enter_context(nc.sbuf_tensor("flag", [1, 1], mybir.dt.int32))
        mem.ident = sb("ident", [P, P])
        mem.group = sb("group", [P, P])
        mem.quad_mean = sb("quad_mean", [P, P])
        mem.tiny = sb("tiny", [P, 1])
        mem.eps_gn = sb("eps_gn", [P, 1])
        mem.minus_tiny, mem.tiny_log = sb("minus_tiny", [P, 1]), sb("tiny_log", [P, 1])
        mem.one, mem.two = (sb(n, [P, HB, PAIRS]) for n in ("one", "two"))
        mem.shift = sb("shift", [P, B])
        mem.even = sb("even", [P, B, N])
        mem.psum = ctx.enter_context(nc.psum_tensor("psum", [P, 8, 512], F32))
        mem.banks = [mem.psum[:, i, :] for i in range(8)]
        mem.dots = mem.banks[0:2]
        Passed.sem = ctx.enter_context(nc.semaphore("passed"))
        constants(nc, mem)
        with ExitStack() as first:
            mem.odd = first.enter_context(nc.sbuf_tensor("odd", [P, B, N], F32))
            with ExitStack() as spectral:
                mem.weights = spectral.enter_context(nc.sbuf_tensor("weights", [P, 2, 2, HB, S], F32))
                mem.work = spectral.enter_context(nc.sbuf_tensor("work", [P, 3, HB * PAIRS * S], F32))
                mem.product = [mem.work[:, 0], mem.work[:, 2]]
                normalise(nc, mem, x_dram)
                jacobi(nc, mem)
                logarithm(nc, mem)
            exponential(nc, mem, dram["gamma"], dram["beta"])
            mem.work = first.enter_context(nc.sbuf_tensor("work2", [P, 2, HB * PAIRS * S], F32))
            back_to_channels(nc, mem, x_dram)
        w = Tiles(sb)
        load_weights(nc, mem, w, dram)
        attention_and_experts(nc, mem, w, out_dram)


INPUTS = dict(x="x", gamma="L0_conv_gamma", beta="L0_conv_beta", wq="L1_attn_Wq", wk="L1_attn_Wk", wv="L1_attn_Wv",
              wo="L1_attn_Wo", bo="L1_attn_bo", gate="L1_ffn_gate_w", thr="L1_ffn_thr_w", fc1="L1_ffn_fc1_w",
              lora_a="L1_ffn_lora_A", lora_b="L1_ffn_lora_B", fc2="L1_ffn_fc2_w")


def kernel(**inputs):
    import numpy as np
    import concourse.bacc as bacc
    from concourse.bass_utils import run_bass_kernel_spmd as run

    nc = bacc.Bacc("TRN2", target_bir_lowering=False, num_devices=1)
    arrays, dram = {}, {}
    for name, source in INPUTS.items():
        arrays[f"in_{name}"] = np.ascontiguousarray(inputs[source])
        dram[name] = nc.dram_tensor(f"in_{name}", arrays[f"in_{name}"].shape, F32, kind="ExternalInput").ap()
    out = nc.dram_tensor("out_0", (B, P, S, S), F32, kind="ExternalOutput").ap()
    hybrid_kernel(nc, dram, out)
    r = run(nc, [arrays], core_ids=[0])
    return r.results[0]["out_0"]
```
